# Optimizing a Trainium2 kernel written in Bass

```python
import numpy as np
import jax
import jax.numpy as jnp

def _softmax(x, axis=-1):
    return jax.nn.softmax(x, axis=axis)

def _gelu(x):
    return jax.nn.gelu(x, approximate=True)

def _silu(x):
    return jax.nn.silu(x)

def _sigmoid(x):
    return jax.nn.sigmoid(x)

def _layernorm(x, axis=-1, eps=1e-05):
    m = jnp.mean(x, axis=axis, keepdims=True)
    v = jnp.var(x, axis=axis, keepdims=True)
    return (x - m) / jnp.sqrt(v + eps)

def _scatter_add(tgt, idx, src, axis=0):
    return tgt.at[idx].add(src)

def _segment_sum(src, seg, n):
    return jax.ops.segment_sum(src, seg, n)
kernel_name = 'mk_adj_preln_d2_adj_r2_1968fb'

def setup_inputs(seed: int=0):
    np.random.seed(seed)
    _w = jnp.asarray

    def _rec_inputs():
        import jax
        import jax.numpy as jnp
        _gk = jax.random.key(seed)
        x = -0.0005207 + 1.001 * jax.random.normal(jax.random.fold_in(_gk, 1), (8192, 128), jnp.float32)
        _a = jax.random.bernoulli(jax.random.fold_in(_gk, 2), 0.000976562, (8192, 8192))
        adj = _a.astype(jnp.int32)
        return (x, adj)
    x, adj = _rec_inputs()

    def _L0_gnn_setup():
        import jax, jax.numpy as jnp
        import numpy as np
        N, D = (4096, 128)
        NEG_BIG = -9000000000000000.0
        key = jax.random.key(seed)
        k1, k2, k3 = jax.random.split(key, 3)
        h = jax.random.normal(k1, (N, D), dtype=jnp.float32)
        adj = jax.random.randint(k2, (N, N), 0, 2, dtype=jnp.int32)
        bound = np.sqrt(6.0 / (2 * D + 1)).astype(np.float32)
        a = jax.random.uniform(k3, (2 * D, 1), dtype=jnp.float32, minval=-bound, maxval=bound)
        return {'h': h, 'adj': adj, 'a': a}
    _L0_gnn_all = _L0_gnn_setup()
    _L0_gnn_in = {k: v for k, v in _L0_gnn_all.items() if k in ('a',)}
    del _L0_gnn_all

    def _L1_gnn_setup():
        import jax, jax.numpy as jnp
        import numpy as np
        N = 4096
        IN_F = 128
        OUT_F = 128
        key = jax.random.key(seed)
        k_v, k_adj, k1, k2, k3, kb = jax.random.split(key, 6)
        stdv = 1.0 / np.sqrt(OUT_F)
        V = jax.random.normal(k_v, (N, IN_F), dtype=jnp.float32)
        adj = jax.random.randint(k_adj, (N, N), 0, 4, dtype=jnp.int32)
        w1 = jax.random.uniform(k1, (IN_F, OUT_F), jnp.float32, -stdv, stdv)
        w2 = jax.random.uniform(k2, (IN_F, OUT_F), jnp.float32, -stdv, stdv)
        w3 = jax.random.uniform(k3, (IN_F, OUT_F), jnp.float32, -stdv, stdv)
        bias = jax.random.uniform(kb, (OUT_F,), jnp.float32, -stdv, stdv)
        return {'V': V, 'adj': adj, 'w1': w1, 'w2': w2, 'w3': w3, 'bias': bias}
    _L1_gnn_all = _L1_gnn_setup()
    _L1_gnn_in = {k: v for k, v in _L1_gnn_all.items() if k in ('w1', 'w2', 'w3', 'bias')}
    del _L1_gnn_all
    return {'x': x, 'adj': adj, 'L0_gnn_a': _L0_gnn_in['a'], 'L1_gnn_w1': _L1_gnn_in['w1'], 'L1_gnn_w2': _L1_gnn_in['w2'], 'L1_gnn_w3': _L1_gnn_in['w3'], 'L1_gnn_bias': _L1_gnn_in['bias']}

def reference(x, adj, L0_gnn_a, L1_gnn_w1, L1_gnn_w2, L1_gnn_w3, L1_gnn_bias):
    import jax
    import jax.numpy as jnp

    def _L0_gnn_ref(h, adj, a):
        import jax, jax.numpy as jnp
        import numpy as np
        N, D = (4096, 128)
        NEG_BIG = -9000000000000000.0
        d = h.shape[1]
        h1 = h @ a[:d]
        h2 = h @ a[d:]
        e = jax.nn.leaky_relu(h1 + h2.T, negative_slope=0.01)
        attention = jnp.where(adj > 0, e, NEG_BIG)
        attention = jax.nn.softmax(attention, axis=1)
        return attention @ h

    def _L1_gnn_ref(V, adj, w1, w2, w3, bias):
        import jax, jax.numpy as jnp
        import numpy as np
        N = 4096
        IN_F = 128
        OUT_F = 128
        o1 = jnp.matmul((adj == 1).astype(jnp.float32), jnp.matmul(V, w1))
        o2 = jnp.matmul((adj == 2).astype(jnp.float32), jnp.matmul(V, w2))
        o3 = jnp.matmul((adj == 3).astype(jnp.float32), jnp.matmul(V, w3))
        return o1 + o2 + o3 + bias
    h = jnp.maximum(_layernorm(x, axis=-1), 0.0)
    x = x + _L0_gnn_ref(h, adj, L0_gnn_a)
    h = jnp.maximum(_layernorm(x, axis=-1), 0.0)
    x = x + _L1_gnn_ref(h, adj, L1_gnn_w1, L1_gnn_w2, L1_gnn_w3, L1_gnn_bias)
    return x

_drawn_inputs = setup_inputs


def setup_inputs(seed=0):
    import zlib

    import numpy as np

    out = dict(_drawn_inputs(seed))
    spreads = {}
    factors = {}
    for name, (base, spread) in spreads.items():
        noise = np.random.default_rng([zlib.crc32(name.encode()), seed]).standard_normal(out[name].shape)
        drawn = base * np.exp(spread * noise) if base else spread * noise
        out[name] = jnp.asarray(drawn.astype(out[name].dtype))
    for name, factor in factors.items():
        out[name] = (out[name] * factor).astype(out[name].dtype)
    return out
```

```python
from contextlib import ExitStack

import concourse.bass as bass
from concourse import mybir

P = 128
N = 8192
D = 128
NT = N // P
WB = 1024
NB = N // WB
TB = WB // P
NPAIR = NT // 2
D1 = D + 1
CH = 4
NCH = NT // CH
LC = 16
NLC = NT // LC
EPS = 1e-5
SLOPE = 0.01
LOW = -3.0e38

F32 = mybir.dt.float32
I32 = mybir.dt.int32
ALU = mybir.AluOpType
ACT = mybir.ActivationFunctionType
AX = mybir.AxisListType.X


class Phase:

    def __init__(self, nc, name):
        self.nc, self.name, self.ctx = nc, name, ExitStack()

    def __enter__(self):
        self.ctx.__enter__()
        return self

    def __exit__(self, *a):
        return self.ctx.__exit__(*a)

    def sb(self, name, shape, dt=F32):
        return self.ctx.enter_context(self.nc.sbuf_tensor(f"{self.name}_{name}", shape, dt))

    def ps(self, name, shape, dt=F32):
        return self.ctx.enter_context(self.nc.psum_tensor(f"{self.name}_{name}", shape, dt))

    def sem(self, name):
        return self.ctx.enter_context(self.nc.semaphore(f"{self.name}_{name}"))


def constants(nc, ph):
    ident = ph.sb("ident", [P, P])
    ones = ph.sb("ones", [P, P])
    cleared, made, filled = ph.sem("cleared"), ph.sem("made"), ph.sem("filled")
    with nc.Block() as block:
        @block.gpsimd
        def _(pool):
            nc.gpsimd.memset(ident[:, :], 0.0).then_inc(cleared, 1)
            pool.wait_ge(cleared, 1)
            nc.gpsimd.affine_select(out=ident[:, :], in_=ident[:, :], compare_op=ALU.not_equal, fill=1.0,
                                    base=0, pattern=[[-1, P]], channel_multiplier=1).then_inc(made, 1)
            pool.wait_ge(made, 1)

        @block.vector
        def _(dve):
            nc.vector.memset(ones[:, :], 1.0).then_inc(filled, 1)
            dve.wait_ge(filled, 1)
    return ident, ones



def normalise(nc, ph, block, src, h, on_pe, on_act, on_dve):
    xs = ph.sb("xs", [P, NT, D])
    sq = ph.sb("sq", [P, 2, LC, D])
    total, mean, var, std, rstd = (ph.sb(n, [P, NT]) for n in ("total", "mean", "var", "std", "rstd"))
    loaded = [ph.sem(f"loaded{c}") for c in range(NLC)]
    summed, averaged, centred, squared, ssq, biased, rooted, inverted, normed = (
        ph.sem(n) for n in ("summed", "averaged", "centred", "squared", "ssq", "biased", "rooted",
                            "inverted", "normed"))
    tiles = src.rearrange("(t p) d -> p t d", p=P)

    def span(c):
        return slice(c * LC, (c + 1) * LC)

    def wide(col, c):
        return col[:, span(c)].unsqueeze(2).to_broadcast([P, LC, D])

    @block.sync
    def _(sp):
        for c in range(NLC):
            sp.dma_start(xs[:, span(c), :], tiles[:, span(c), :]).then_inc(loaded[c], 16)

    @block.scalar
    def _(act):
        for c in range(NLC):
            act.wait_ge(centred, c + 1)
            if c >= 2:
                act.wait_ge(ssq, c - 1)
            nc.scalar.activation(sq[:, c % 2], xs[:, span(c), :], ACT.Square).then_inc(squared, 1)
        act.wait_ge(biased, 1)
        nc.scalar.activation(std[:, :], var[:, :], ACT.Sqrt).then_inc(rooted, 1)
        on_act(act, normed)

    @block.vector
    def _(dve):
        for c in range(NLC):
            dve.wait_ge(loaded[c], 16)
            nc.vector.reduce_sum(total[:, span(c)], xs[:, span(c), :], AX).then_inc(summed, 1)
            dve.wait_ge(summed, c + 1)
            nc.vector.tensor_scalar(mean[:, span(c)], total[:, span(c)], 1.0 / D, None,
                                    ALU.mult).then_inc(averaged, 1)
            dve.wait_ge(averaged, c + 1)
            nc.vector.tensor_tensor(xs[:, span(c), :], xs[:, span(c), :], wide(mean, c),
                                    ALU.subtract).then_inc(centred, 1)
        for c in range(NLC):
            dve.wait_ge(squared, c + 1)
            nc.vector.reduce_sum(total[:, span(c)], sq[:, c % 2], AX).then_inc(ssq, 1)
        dve.wait_ge(ssq, NLC)
        nc.vector.tensor_scalar(var[:, :], total[:, :], 1.0 / D, EPS, ALU.mult, ALU.add).then_inc(biased, 1)
        dve.wait_ge(rooted, 1)
        nc.vector.reciprocal(rstd[:, :], std[:, :]).then_inc(inverted, 1)
        dve.wait_ge(inverted, 1)
        dve.wait_ge(centred, NLC)
        for c in range(NLC):
            nc.vector.scalar_tensor_tensor(out=h[:, span(c), 0:D], in0=xs[:, span(c), :], scalar=0.0,
                                           in1=wide(rstd, c), op0=ALU.max, op1=ALU.mult).then_inc(normed, 1)
        on_dve(dve, normed)

    @block.tensor
    def _(pe):
        on_pe(pe, normed)


def scores_phase(nc, ident, ones, x, a2, h, h1c, h2c, h1b, mean_h):
    with Phase(nc, "sc") as ph:
        aw = ph.sb("aw", [D, 2])
        a1w = ph.sb("a1w", [D, P])
        nth = ph.sb("nth", [P, P])
        hT = ph.sb("hT", [D, 2, CH * P])
        pT = ph.ps("pT", [D, 2, CH * P])
        pH = ph.ps("pH", [P, 2, 512])
        pB = ph.ps("pB", [P, 2, CH * P])
        pM = ph.ps("pM", [P, 512])
        a_in, a_wide, turned, hT_ready, projected, spread, taken, copied, averaged_h = (
            ph.sem(n) for n in ("a_in", "a_wide", "turned", "hT_ready", "projected", "spread", "taken",
                                "copied", "averaged_h"))
        mean_out = ph.sem("mean_out")
        with nc.Block() as block:
            def on_pe(pe, normed):
                pe.wait_ge(a_wide, 3)
                for k in range(NCH + 1):
                    if k < NCH:
                        pe.wait_ge(normed, k * CH // LC + 1)
                        if k >= 2:
                            pe.wait_ge(hT_ready, k - 1)
                        for t in range(CH):
                            last = nc.tensor.transpose(pT[:, k % 2, t * P:(t + 1) * P],
                                                       h[:, k * CH + t, 0:D], ident[:, :])
                        last.then_inc(turned, 1)
                        for t in range(CH):
                            n = k * CH + t
                            last = nc.tensor.matmul(pM[:, 0:D], nth[:, :], h[:, n, 0:D],
                                                    start=(n == 0), stop=(n == NT - 1))
                    if k == NCH - 1:
                        last.then_inc(averaged_h, 1)
                    if k >= 1:
                        c = k - 1
                        pe.wait_ge(hT_ready, c + 1)
                        if c >= 2:
                            pe.wait_ge(taken, c - 1)
                            pe.wait_ge(copied, c - 1)
                        for t in range(CH):
                            last = nc.tensor.matmul(pH[:, c % 2, 2 * t:2 * t + 2],
                                                    hT[:, c % 2, t * P:(t + 1) * P], aw[:, :],
                                                    start=True, stop=True)
                        last.then_inc(projected, 1)
                        nc.tensor.matmul(pB[:, c % 2, :], a1w[:, :], hT[:, c % 2, :],
                                         start=True, stop=True).then_inc(spread, 1)

            def on_act(act, normed):
                for k in range(NCH + 1):
                    if k < NCH:
                        act.wait_ge(turned, k + 1)
                        if k >= 2:
                            act.wait_ge(spread, k - 1)
                        nc.scalar.activation(hT[:, k % 2, :], pT[:, k % 2, :], ACT.Copy).then_inc(hT_ready, 1)
                    if k >= 1:
                        act.wait_ge(spread, k)
                        nc.scalar.activation(h1b[:, (k - 1) * CH * P:k * CH * P], pB[:, (k - 1) % 2, :],
                                             ACT.Copy).then_inc(copied, 1)

            def on_dve(dve, normed):
                nc.vector.memset(h[:, :, D:D1], 1.0).then_inc(mean_out, 1)
                for c in range(NCH):
                    dve.wait_ge(projected, c + 1)
                    got = pH[:, c % 2, 0:2 * CH].rearrange("p (t k) -> p t k", k=2)
                    nc.vector.tensor_copy(h1c[:, c * CH:(c + 1) * CH], got[:, :, 0])
                    nc.vector.tensor_copy(h2c[:, c * CH:(c + 1) * CH], got[:, :, 1]).then_inc(taken, 1)
                dve.wait_ge(averaged_h, 1)
                nc.vector.tensor_copy(mean_h[:, :], pM[:, 0:D]).then_inc(mean_out, 1)
                dve.wait_ge(mean_out, 2)
                dve.wait_ge(taken, NCH)

            @block.gpsimd
            def _(pool):
                pool.dma_start(aw[:, :], a2).then_inc(a_in, 16)
                pool.wait_ge(a_in, 16)
                nc.gpsimd.tensor_scalar(a1w[:, :], ones[:, :], aw[:, 0:1], None, ALU.mult).then_inc(a_wide, 1)
                nc.gpsimd.memset(nth[:, :], 1.0 / N).then_inc(a_wide, 2)

            normalise(nc, ph, block, x, h, on_pe, on_act, on_dve)


def general_maxima(nc, ident, ones, adjT, h1c, h2c, mb):
    with Phase(nc, "mx") as ph:
        adj = ph.sb("adj", [P, 2, WB], I32)
        off = ph.sb("off", [P, 2, WB])
        best = ph.sb("best", [P, WB])
        top = ph.sb("top", [P, NT])
        s = ph.sb("s", [P, NT])
        m = ph.sb("m", [P, NT])
        diag = ph.sb("diag", [P, 2, P])
        pR = ph.ps("pR", [P, TB, 128])
        pD = ph.ps("pD", [P, 2, 512])
        adj_in = [ph.sem(f"adj_in{b}") for b in range(2)]
        adj_used = [ph.sem(f"adj_used{b}") for b in range(2)]
        best_set, turned, topped, m_ready = (
            ph.sem(n) for n in ("best_set", "turned", "topped", "m_ready"))
        diag_ready = [ph.sem(f"diag_ready{b}") for b in range(2)]
        diag_used = [ph.sem(f"diag_used{b}") for b in range(2)]
        row_out = [ph.sem(f"row_out{b}") for b in range(2)]
        with nc.Block() as block:
            @block.sync
            def _(sp):
                for b in range(2):
                    sp.sem_inc(adj_used[b], 1)
                with sp.Fori(0, NB) as i:
                    with sp.Fori(0, NPAIR) as q:
                        for b in range(2):
                            sp.wait_ge(adj_used[b], i * NPAIR + q + 1)
                            sp.dma_start(adj[:, b, :], adjT[bass.ds((q * 2 + b) * P, P), bass.ds(i * WB, WB)]
                                         ).then_inc(adj_in[b], 16)

            @block.vector
            def _(dve):
                dve.sem_inc(turned, 1)
                for b in range(2):
                    dve.sem_inc(diag_used[b], 1)
                with dve.Fori(0, NB) as i:
                    dve.wait_ge(turned, i + 1)
                    nc.vector.memset(best[:, :], LOW).then_inc(best_set, 1)
                    with dve.Fori(0, NPAIR) as q:
                        for b in range(2):
                            dve.wait_ge(adj_in[b], (i * NPAIR + q + 1) * 16)
                            nc.vector.tensor_scalar(off[:, b, :], adj[:, b, :], 0.0, LOW, ALU.is_le,
                                                    ALU.mult).then_inc(adj_used[b], 1)
                            dve.wait_ge(adj_used[b], i * NPAIR + q + 2)
                            dve.wait_ge(best_set, i * (2 * NPAIR + 1) + q * 2 + b + 1)
                            nc.vector.scalar_tensor_tensor(
                                out=best[:, :], in0=off[:, b, :], scalar=h2c[:, bass.ds(q * 2 + b, 1)],
                                in1=best[:, :], op0=ALU.add, op1=ALU.max).then_inc(best_set, 1)
                    dve.wait_ge(turned, i + 2)
                    nc.vector.reduce_max(top[:, bass.ds(i * TB, TB)], pR[:, :, :], AX).then_inc(topped, 1)
                dve.wait_ge(topped, NB + 1)
                nc.vector.tensor_tensor(s[:, :], h1c[:, :], top[:, :], ALU.add).then_inc(m_ready, 1)
                dve.wait_ge(m_ready, 1)
                nc.vector.scalar_tensor_tensor(out=m[:, :], in0=s[:, :], scalar=SLOPE, in1=s[:, :],
                                               op0=ALU.mult, op1=ALU.max).then_inc(m_ready, 1)
                dve.wait_ge(m_ready, 2)
                with dve.Fori(0, NPAIR) as q:
                    for b in range(2):
                        dve.wait_ge(diag_used[b], q + 1)
                        nc.vector.tensor_scalar(diag[:, b, :], ident[:, :], m[:, bass.ds(q * 2 + b, 1)], None,
                                                ALU.mult).then_inc(diag_ready[b], 1)

            @block.tensor
            def _(pe):
                pe.sem_inc(topped, 1)
                for b in range(2):
                    pe.sem_inc(row_out[b], 1)
                with pe.Fori(0, NB) as i:
                    pe.wait_ge(best_set, (i + 1) * (2 * NPAIR + 1))
                    pe.wait_ge(topped, i + 1)
                    for t in range(TB):
                        last = nc.tensor.transpose(pR[:, t, :], best[:, t * P:(t + 1) * P], ident[:, :])
                    last.then_inc(turned, 1)
                with pe.Fori(0, NPAIR) as q:
                    for b in range(2):
                        pe.wait_ge(diag_ready[b], q + 1)
                        pe.wait_ge(row_out[b], q + 1)
                        nc.tensor.matmul(pD[:, b, 0:P], ones[:, :], diag[:, b, :], start=True,
                                         stop=True).then_inc(diag_used[b], 1)

            @block.scalar
            def _(act):
                with act.Fori(0, NPAIR) as q:
                    for b in range(2):
                        act.wait_ge(diag_used[b], q + 2)
                        nc.scalar.activation(mb[:, bass.ds((q * 2 + b) * P, P)], pD[:, b, 0:P],
                                             ACT.Copy).then_inc(row_out[b], 1)


def general_attention(nc, x, adjT, h, h2c, h1b, mb, mean_h, x1):
    with Phase(nc, "at") as ph:
        adj = ph.sb("adj", [P, 2, WB], I32)
        z = ph.sb("z", [P, 2, WB])
        e = ph.sb("e", [P, 2, WB])
        dd = ph.sb("dd", [P, 2, WB])
        below = ph.sb("below", [P, 2, WB])
        w = ph.sb("w", [P, 2, WB])
        pw = ph.sb("pw", [P, 2, WB])
        acc = ph.ps("acc", [P, TB, 512])
        num = ph.sb("num", [P, TB, D1])
        alone, den, inv = (ph.sb(n, [P, TB]) for n in ("alone", "den", "inv"))
        part = ph.sb("part", [P, TB, D])
        mh = ph.sb("mh", [P, TB, D])
        xin = ph.sb("xin", [P, TB, D])
        adj_in = [ph.sem(f"adj_in{b}") for b in range(2)]
        w_ready = [ph.sem(f"w_ready{b}") for b in range(2)]
        d_ready = [ph.sem(f"d_ready{b}") for b in range(2)]
        b_ready = [ph.sem(f"b_ready{b}") for b in range(2)]
        p_ready = [ph.sem(f"p_ready{b}") for b in range(2)]
        p_used = [ph.sem(f"p_used{b}") for b in range(2)]
        z_ready, e_ready, drained, fin, x_in, x_out = (
            ph.sem(n) for n in ("z_ready", "e_ready", "drained", "fin", "x_in", "x_out"))
        FIN = 7
        xt = x.rearrange("(i t p) d -> i p t d", p=P, t=TB)
        x1t = x1.rearrange("(i t p) d -> i p t d", p=P, t=TB)
        with nc.Block() as block:
            @block.sync
            def _(sp):
                for b in range(2):
                    sp.sem_inc(p_ready[b], 1)
                with sp.Fori(0, NB) as i:
                    with sp.Fori(0, NPAIR) as q:
                        for b in range(2):
                            sp.wait_ge(p_ready[b], i * NPAIR + q + 1)
                            sp.dma_start(adj[:, b, :], adjT[bass.ds((q * 2 + b) * P, P), bass.ds(i * WB, WB)]
                                         ).then_inc(adj_in[b], 16)

            @block.scalar
            def _(act):
                act.sem_inc(fin, 1)
                with act.Fori(0, NB) as i:
                    act.wait_ge(fin, i * FIN + 1)
                    act.dma_start(xin[:, :, :], xt[bass.ds(i, 1), :, :, :].squeeze(0)).then_inc(x_in, 16)
                    with act.Fori(0, NPAIR) as q:
                        for b in range(2):
                            n = i * NPAIR + q
                            act.wait_ge(d_ready[b], n + 1)
                            nc.scalar.activation(below[:, b, :], dd[:, b, :], ACT.Relu,
                                                 scale=-1.0).then_inc(b_ready[b], 1)
                            act.wait_ge(b_ready[b], n + 2)
                            act.wait_ge(p_ready[b], n + 1)
                            nc.scalar.activation(w[:, b, :], below[:, b, :], ACT.Exp,
                                                 scale=-1.0).then_inc(w_ready[b], 1)
                    act.wait_ge(fin, (i + 1) * FIN + 1)
                    act.dma_start(x1t[bass.ds(i, 1), :, :, :].squeeze(0), part[:, :, :]).then_inc(x_out, 16)
                    act.wait_ge(x_out, (i + 1) * 16)

            @block.vector
            def _(dve):
                for b in range(2):
                    dve.sem_inc(b_ready[b], 1)
                    dve.sem_inc(p_used[b], 1)
                with dve.Fori(0, NB) as i:
                    with dve.Fori(0, NPAIR) as q:
                        for b in range(2):
                            n = i * NPAIR + q
                            cols = bass.ds(i * WB, WB)
                            nc.vector.tensor_scalar(z[:, b, :], h1b[:, cols], h2c[:, bass.ds(q * 2 + b, 1)], None,
                                                    ALU.add).then_inc(z_ready, 1)
                            dve.wait_ge(z_ready, n * 2 + b + 1)
                            nc.vector.scalar_tensor_tensor(out=e[:, b, :], in0=z[:, b, :], scalar=SLOPE,
                                                           in1=z[:, b, :], op0=ALU.mult,
                                                           op1=ALU.max).then_inc(e_ready, 1)
                            dve.wait_ge(e_ready, n * 2 + b + 1)
                            dve.wait_ge(b_ready[b], n + 1)
                            nc.vector.tensor_tensor(dd[:, b, :], e[:, b, :], mb[:, cols],
                                                    ALU.subtract).then_inc(d_ready[b], 1)
                        for b in range(2):
                            n = i * NPAIR + q
                            dve.wait_ge(w_ready[b], n + 1)
                            dve.wait_ge(adj_in[b], (n + 1) * 16)
                            dve.wait_ge(p_used[b], n + 1)
                            nc.vector.scalar_tensor_tensor(out=pw[:, b, :], in0=adj[:, b, :], scalar=0.0,
                                                           in1=w[:, b, :], op0=ALU.is_gt,
                                                           op1=ALU.mult).then_inc(p_ready[b], 1)
                    dve.wait_ge(p_used[1], (i + 1) * NPAIR + 1)
                    nc.vector.tensor_copy(num[:, :, :], acc[:, :, 0:D1]).then_inc(drained, 1)
                    dve.wait_ge(drained, i + 2)
                    nc.vector.tensor_scalar(alone[:, :], num[:, :, D], 0.0, None, ALU.is_equal).then_inc(fin, 1)
                    dve.wait_ge(fin, i * FIN + 2)
                    nc.vector.tensor_tensor(den[:, :], num[:, :, D], alone[:, :], ALU.add).then_inc(fin, 1)
                    dve.wait_ge(fin, i * FIN + 3)
                    nc.vector.reciprocal(inv[:, :], den[:, :]).then_inc(fin, 1)
                    dve.wait_ge(fin, i * FIN + 4)
                    dve.wait_ge(x_in, (i + 1) * 16)
                    nc.vector.tensor_tensor(part[:, :, :], num[:, :, 0:D],
                                            inv[:, :].unsqueeze(2).to_broadcast([P, TB, D]), ALU.mult).then_inc(fin, 1)
                    nc.vector.tensor_tensor(mh[:, :, :], alone[:, :].unsqueeze(2).to_broadcast([P, TB, D]),
                                            mean_h[:, :].unsqueeze(1).to_broadcast([P, TB, D]),
                                            ALU.mult).then_inc(fin, 1)
                    dve.wait_ge(fin, i * FIN + 6)
                    nc.vector.tensor_tensor(part[:, :, :], part[:, :, :], mh[:, :, :], ALU.add).then_inc(fin, 1)
                    dve.wait_ge(fin, i * FIN + 7)
                    nc.vector.tensor_tensor(part[:, :, :], part[:, :, :], xin[:, :, :], ALU.add).then_inc(fin, 1)

            @block.tensor
            def _(pe):
                def step(i, q, b, first):
                    pe.wait_ge(p_ready[b], i * NPAIR + q + 2)
                    for t in range(TB):
                        last = nc.tensor.matmul(acc[:, t, 0:D1], pw[:, b, t * P:(t + 1) * P],
                                                h[:, bass.ds(q * 2 + b, 1), :].squeeze(1), start=first, stop=False,
                                                skip_group_check=True)
                    last.then_inc(p_used[b], 1)

                pe.sem_inc(drained, 1)
                with pe.Fori(0, NB) as i:
                    pe.wait_ge(drained, i + 1)
                    step(i, 0, 0, True)
                    step(i, 0, 1, False)
                    with pe.Fori(1, NPAIR) as q:
                        for b in range(2):
                            step(i, q, b, False)


def values_phase(nc, ident, x1, ws, h, vw):
    K = len(ws)
    with Phase(nc, "va") as ph:
        wt = ph.sb("wt", [D, K, D])
        hT = ph.sb("hT", [D, 2, CH * P])
        pT = ph.ps("pT", [D, 2, CH * P])
        pV = ph.ps("pV", [P, CH, 512])
        w_in, turned, hT_ready, projected, taken = (
            ph.sem(n) for n in ("w_in", "turned", "hT_ready", "projected", "taken"))
        with nc.Block() as block:
            def on_pe(pe, normed):
                pe.wait_ge(w_in, 16 * K)
                for k in range(NCH + 1):
                    if k < NCH:
                        pe.wait_ge(normed, k * CH // LC + 1)
                        if k >= 2:
                            pe.wait_ge(hT_ready, k - 1)
                        for t in range(CH):
                            last = nc.tensor.transpose(pT[:, k % 2, t * P:(t + 1) * P],
                                                       h[:, k * CH + t, 0:D], ident[:, :])
                        last.then_inc(turned, 1)
                    if k >= 1:
                        c = k - 1
                        pe.wait_ge(hT_ready, c + 1)
                        for t in range(CH):
                            if c >= 1:
                                pe.wait_ge(taken, (c - 1) * CH + t + 1)
                            nc.tensor.matmul(pV[:, t, 0:K * D], hT[:, c % 2, t * P:(t + 1) * P],
                                             wt[:, :, :].rearrange("p k d -> p (k d)"),
                                             start=True, stop=True).then_inc(projected, 1)

            def on_act(act, normed):
                for k in range(NCH):
                    act.wait_ge(turned, k + 1)
                    if k >= 2:
                        act.wait_ge(projected, (k - 1) * CH)
                    nc.scalar.activation(hT[:, k % 2, :], pT[:, k % 2, :], ACT.Copy).then_inc(hT_ready, 1)

            def on_dve(dve, normed):
                for n in range(NT):
                    dve.wait_ge(projected, n + 1)
                    nc.vector.tensor_copy(vw[:, n, :, :].rearrange("p k d -> p (k d)"),
                                          pV[:, n % CH, 0:K * D]).then_inc(taken, 1)
                dve.wait_ge(taken, NT)

            @block.gpsimd
            def _(pool):
                for k in range(K):
                    pool.dma_start(wt[:, k, :], ws[k]).then_inc(w_in, 16)

            normalise(nc, ph, block, x1, h, on_pe, on_act, on_dve)


def general_kinds(nc, adjT, vw, x1, bias, out):
    K = 3
    with Phase(nc, "ki") as ph:
        adj = ph.sb("adj", [P, 2, WB], I32)
        mask = ph.sb("mask", [P, 2, K, WB])
        acc = ph.ps("acc", [P, TB, 512])
        res = ph.sb("res", [P, TB, D])
        xin = ph.sb("xin", [P, TB, D])
        brow = ph.sb("brow", [P, D])
        adj_in = [ph.sem(f"adj_in{b}") for b in range(2)]
        m_ready = [ph.sem(f"m_ready{b}") for b in range(2)]
        m_used = [ph.sem(f"m_used{b}") for b in range(2)]
        b_in, fin, x_in, x_out = (ph.sem(n) for n in ("b_in", "fin", "x_in", "x_out"))
        FIN = 2
        x1t = x1.rearrange("(i t p) d -> i p t d", p=P, t=TB)
        ot = out.rearrange("(i t p) d -> i p t d", p=P, t=TB)
        with nc.Block() as block:
            @block.sync
            def _(sp):
                for b in range(2):
                    sp.sem_inc(m_ready[b], 1)
                sp.dma_start(brow[:, :], bias.partition_broadcast(P)).then_inc(b_in, 16)
                with sp.Fori(0, NB) as i:
                    with sp.Fori(0, NPAIR) as q:
                        for b in range(2):
                            sp.wait_ge(m_ready[b], (i * NPAIR + q) * K + 1)
                            sp.dma_start(adj[:, b, :], adjT[bass.ds((q * 2 + b) * P, P), bass.ds(i * WB, WB)]
                                         ).then_inc(adj_in[b], 16)

            @block.scalar
            def _(act):
                act.sem_inc(fin, 1)
                with act.Fori(0, NB) as i:
                    act.wait_ge(fin, i * FIN + 1)
                    act.dma_start(xin[:, :, :], x1t[bass.ds(i, 1), :, :, :].squeeze(0)).then_inc(x_in, 16)
                    act.wait_ge(fin, (i + 1) * FIN + 1)
                    act.dma_start(ot[bass.ds(i, 1), :, :, :].squeeze(0), res[:, :, :]).then_inc(x_out, 16)
                    act.wait_ge(x_out, (i + 1) * 16)

            @block.vector
            def _(dve):
                for b in range(2):
                    dve.sem_inc(m_used[b], 1)
                dve.wait_ge(b_in, 16)
                with dve.Fori(0, NB) as i:
                    with dve.Fori(0, NPAIR) as q:
                        for b in range(2):
                            n = i * NPAIR + q
                            dve.wait_ge(adj_in[b], (n + 1) * 16)
                            dve.wait_ge(m_used[b], n + 1)
                            for k in range(K):
                                nc.vector.tensor_scalar(mask[:, b, k, :], adj[:, b, :], float(k + 1), None,
                                                        ALU.is_equal).then_inc(m_ready[b], 1)
                    dve.wait_ge(m_used[1], (i + 1) * NPAIR + 1)
                    dve.wait_ge(x_in, (i + 1) * 16)
                    nc.vector.tensor_tensor(res[:, :, :], acc[:, :, 0:D], xin[:, :, :], ALU.add).then_inc(fin, 1)
                    dve.wait_ge(fin, i * FIN + 2)
                    nc.vector.tensor_tensor(res[:, :, :], res[:, :, :],
                                            brow[:, :].unsqueeze(1).to_broadcast([P, TB, D]),
                                            ALU.add).then_inc(fin, 1)

            @block.tensor
            def _(pe):
                def step(i, q, b, first):
                    pe.wait_ge(m_ready[b], (i * NPAIR + q + 1) * K + 1)
                    for t in range(TB):
                        for k in range(K):
                            last = nc.tensor.matmul(acc[:, t, 0:D], mask[:, b, k, t * P:(t + 1) * P],
                                                    vw[:, bass.ds(q * 2 + b, 1), k, :].squeeze(1),
                                                    start=(first and k == 0), stop=False, skip_group_check=True)
                    last.then_inc(m_used[b], 1)

                with pe.Fori(0, NB) as i:
                    pe.wait_ge(fin, i * FIN + 1)
                    step(i, 0, 0, True)
                    step(i, 0, 1, False)
                    with pe.Fori(1, NPAIR) as q:
                        for b in range(2):
                            step(i, q, b, False)


def general_layers(nc, x, adjT, a2, ws, bias, x1, out):
    with Phase(nc, "ge") as ph:
        ident, ones = constants(nc, ph)
        with Phase(nc, "g0") as p0:
            h = p0.sb("h", [P, NT, D1])
            h1c, h2c = p0.sb("h1c", [P, NT]), p0.sb("h2c", [P, NT])
            mean_h = p0.sb("mean_h", [P, D])
            h1b = p0.sb("h1b", [P, N])
            scores_phase(nc, ident, ones, x, a2, h, h1c, h2c, h1b, mean_h)
            mb = p0.sb("mb", [P, N])
            general_maxima(nc, ident, ones, adjT, h1c, h2c, mb)
            general_attention(nc, x, adjT, h, h2c, h1b, mb, mean_h, x1)
        with Phase(nc, "g1") as p1:
            vw = p1.sb("vw", [P, NT, 3, D])
            with Phase(nc, "g2") as p2:
                h = p2.sb("h", [P, NT, D])
                values_phase(nc, ident, x1, ws, h, vw)
            general_kinds(nc, adjT, vw, x1, bias, out)


def graph_layers(nc, x, adjT, a2, w1, w2, w3, bias, out):
    x1 = nc.dram_tensor("x1_scratch", (N, D), F32, kind="Internal").ap()
    general_layers(nc, x, adjT, a2, [w1, w2, w3], bias, x1, out)


def kernel(x, adj, L0_gnn_a, L1_gnn_w1, L1_gnn_w2, L1_gnn_w3, L1_gnn_bias):
    import numpy as np
    import concourse.bacc as bacc
    from concourse.bass_utils import run_bass_kernel_spmd

    arrays = {
        "x": np.ascontiguousarray(x),
        "adjT": np.ascontiguousarray(np.asarray(adj).T),
        "a2": np.ascontiguousarray(np.asarray(L0_gnn_a).reshape(2, D).T),
        "w1": np.ascontiguousarray(L1_gnn_w1),
        "w2": np.ascontiguousarray(L1_gnn_w2),
        "w3": np.ascontiguousarray(L1_gnn_w3),
        "bias": np.ascontiguousarray(L1_gnn_bias),
    }
    nc = bacc.Bacc("TRN2", target_bir_lowering=False, num_devices=1)
    aps = {k: nc.dram_tensor(f"in_{k}", v.shape, mybir.dt.from_np(v.dtype), kind="ExternalInput").ap()
           for k, v in arrays.items()}
    out = nc.dram_tensor("out", (N, D), F32, kind="ExternalOutput").ap()
    graph_layers(nc, aps["x"], aps["adjT"], aps["a2"], aps["w1"], aps["w2"], aps["w3"], aps["bias"], out)
    r = run_bass_kernel_spmd(nc, [{f"in_{k}": v for k, v in arrays.items()}], core_ids=[0])
    return r.results[0]["out"]
```

```python
from contextlib import ExitStack

import concourse.bass as bass
from concourse import mybir

P = 128
N = 8192
D = 128
NT = N // P
WB = 1024
NB = N // WB
TB = WB // P
GT = 4
NG = NT // GT
GW = GT * WB
NPAIR = NT // 2
MP = NB * NG // 2
D1 = D + 1
CH = 4
NCH = NT // CH
LC = 16
NLC = NT // LC
EPS = 1e-5
SLOPE = 0.01
SPREAD = 8.0
SCALE = 4096.0
LOW = -3.0e38

F32 = mybir.dt.float32
F16 = mybir.dt.float16
BF16 = mybir.dt.bfloat16
F8 = mybir.dt.float8e4
U8 = mybir.dt.uint8
I32 = mybir.dt.int32
ALU = mybir.AluOpType
ACT = mybir.ActivationFunctionType
AX = mybir.AxisListType.X


class Phase:

    def __init__(self, nc, name):
        self.nc, self.name, self.ctx = nc, name, ExitStack()

    def __enter__(self):
        self.ctx.__enter__()
        return self

    def __exit__(self, *a):
        return self.ctx.__exit__(*a)

    def sb(self, name, shape, dt=F32):
        return self.ctx.enter_context(self.nc.sbuf_tensor(f"{self.name}_{name}", shape, dt))

    def ps(self, name, shape, dt=F32):
        return self.ctx.enter_context(self.nc.psum_tensor(f"{self.name}_{name}", shape, dt))

    def sem(self, name):
        return self.ctx.enter_context(self.nc.semaphore(f"{self.name}_{name}"))


def constants(nc, ph):
    ident = ph.sb("ident", [P, P])
    ones = ph.sb("ones", [P, P])
    cleared, made, filled = ph.sem("cleared"), ph.sem("made"), ph.sem("filled")
    with nc.Block() as block:
        @block.gpsimd
        def _(pool):
            nc.gpsimd.memset(ident[:, :], 0.0).then_inc(cleared, 1)
            pool.wait_ge(cleared, 1)
            nc.gpsimd.affine_select(out=ident[:, :], in_=ident[:, :], compare_op=ALU.not_equal, fill=1.0,
                                    base=0, pattern=[[-1, P]], channel_multiplier=1).then_inc(made, 1)
            pool.wait_ge(made, 1)

        @block.vector
        def _(dve):
            nc.vector.memset(ones[:, :], 1.0).then_inc(filled, 1)
            dve.wait_ge(filled, 1)
    return ident, ones



def normalise(nc, ph, block, src, h, on_pe, on_act, on_dve):
    xs = ph.sb("xs", [P, NT, D])
    sq = ph.sb("sq", [P, 2, LC, D])
    total, mean, var, std, rstd = (ph.sb(n, [P, NT]) for n in ("total", "mean", "var", "std", "rstd"))
    loaded = [ph.sem(f"loaded{c}") for c in range(NLC)]
    summed, averaged, centred, squared, ssq, biased, rooted, inverted, normed = (
        ph.sem(n) for n in ("summed", "averaged", "centred", "squared", "ssq", "biased", "rooted",
                            "inverted", "normed"))
    tiles = src.rearrange("(t p) d -> p t d", p=P)

    def span(c):
        return slice(c * LC, (c + 1) * LC)

    def wide(col, c):
        return col[:, span(c)].unsqueeze(2).to_broadcast([P, LC, D])

    @block.sync
    def _(sp):
        for c in range(NLC):
            sp.dma_start(xs[:, span(c), :], tiles[:, span(c), :]).then_inc(loaded[c], 16)

    @block.scalar
    def _(act):
        for c in range(NLC):
            act.wait_ge(centred, c + 1)
            if c >= 2:
                act.wait_ge(ssq, c - 1)
            nc.scalar.activation(sq[:, c % 2], xs[:, span(c), :], ACT.Square).then_inc(squared, 1)
        act.wait_ge(biased, 1)
        nc.scalar.activation(std[:, :], var[:, :], ACT.Sqrt).then_inc(rooted, 1)
        on_act(act, normed)

    @block.vector
    def _(dve):
        for c in range(NLC):
            dve.wait_ge(loaded[c], 16)
            nc.vector.reduce_sum(total[:, span(c)], xs[:, span(c), :], AX).then_inc(summed, 1)
            dve.wait_ge(summed, c + 1)
            nc.vector.tensor_scalar(mean[:, span(c)], total[:, span(c)], 1.0 / D, None,
                                    ALU.mult).then_inc(averaged, 1)
            dve.wait_ge(averaged, c + 1)
            nc.vector.tensor_tensor(xs[:, span(c), :], xs[:, span(c), :], wide(mean, c),
                                    ALU.subtract).then_inc(centred, 1)
        for c in range(NLC):
            dve.wait_ge(squared, c + 1)
            nc.vector.reduce_sum(total[:, span(c)], sq[:, c % 2], AX).then_inc(ssq, 1)
        dve.wait_ge(ssq, NLC)
        nc.vector.tensor_scalar(var[:, :], total[:, :], 1.0 / D, EPS, ALU.mult, ALU.add).then_inc(biased, 1)
        dve.wait_ge(rooted, 1)
        nc.vector.reciprocal(rstd[:, :], std[:, :]).then_inc(inverted, 1)
        dve.wait_ge(inverted, 1)
        dve.wait_ge(centred, NLC)
        for c in range(NLC):
            nc.vector.scalar_tensor_tensor(out=h[:, span(c), 0:D], in0=xs[:, span(c), :], scalar=0.0,
                                           in1=wide(rstd, c), op0=ALU.max, op1=ALU.mult).then_inc(normed, 1)
        on_dve(dve, normed)

    @block.tensor
    def _(pe):
        on_pe(pe, normed)


def scores_phase(nc, name, ident, ones, x, a2, h, h1c, h2c, h1b, mean_h):
    with Phase(nc, name) as ph:
        aw = ph.sb("aw", [D, 2])
        a1w = ph.sb("a1w", [D, P])
        nth = ph.sb("nth", [P, P])
        hT = ph.sb("hT", [D, 2, CH * P])
        pT = ph.ps("pT", [D, 2, CH * P])
        pH = ph.ps("pH", [P, 2, 512])
        pB = ph.ps("pB", [P, 2, CH * P])
        pM = ph.ps("pM", [P, 512])
        a_in, a_wide, turned, hT_ready, projected, spread, taken, copied, averaged_h = (
            ph.sem(n) for n in ("a_in", "a_wide", "turned", "hT_ready", "projected", "spread", "taken",
                                "copied", "averaged_h"))
        mean_out = ph.sem("mean_out")
        with nc.Block() as block:
            def on_pe(pe, normed):
                pe.wait_ge(a_wide, 3)
                for k in range(NCH + 1):
                    if k < NCH:
                        pe.wait_ge(normed, k * CH // LC + 1)
                        if k >= 2:
                            pe.wait_ge(hT_ready, k - 1)
                        for t in range(CH):
                            last = nc.tensor.transpose(pT[:, k % 2, t * P:(t + 1) * P],
                                                       h[:, k * CH + t, 0:D], ident[:, :])
                        last.then_inc(turned, 1)
                        for t in range(CH):
                            n = k * CH + t
                            last = nc.tensor.matmul(pM[:, 0:D], nth[:, :], h[:, n, 0:D],
                                                    start=(n == 0), stop=(n == NT - 1))
                    if k == NCH - 1:
                        last.then_inc(averaged_h, 1)
                    if k >= 1:
                        c = k - 1
                        pe.wait_ge(hT_ready, c + 1)
                        if c >= 2:
                            pe.wait_ge(taken, c - 1)
                            pe.wait_ge(copied, c - 1)
                        for t in range(CH):
                            last = nc.tensor.matmul(pH[:, c % 2, 2 * t:2 * t + 2],
                                                    hT[:, c % 2, t * P:(t + 1) * P], aw[:, :],
                                                    start=True, stop=True)
                        last.then_inc(projected, 1)
                        nc.tensor.matmul(pB[:, c % 2, :], a1w[:, :], hT[:, c % 2, :],
                                         start=True, stop=True).then_inc(spread, 1)

            def on_act(act, normed):
                for k in range(NCH + 1):
                    if k < NCH:
                        act.wait_ge(turned, k + 1)
                        if k >= 2:
                            act.wait_ge(spread, k - 1)
                        nc.scalar.activation(hT[:, k % 2, :], pT[:, k % 2, :], ACT.Copy).then_inc(hT_ready, 1)
                    if k >= 1:
                        act.wait_ge(spread, k)
                        nc.scalar.activation(h1b[:, (k - 1) * CH * P:k * CH * P], pB[:, (k - 1) % 2, :],
                                             ACT.Copy).then_inc(copied, 1)

            def on_dve(dve, normed):
                nc.vector.memset(h[:, :, D:D1], 1.0).then_inc(mean_out, 1)
                for c in range(NCH):
                    dve.wait_ge(projected, c + 1)
                    got = pH[:, c % 2, 0:2 * CH].rearrange("p (t k) -> p t k", k=2)
                    nc.vector.tensor_copy(h1c[:, c * CH:(c + 1) * CH], got[:, :, 0])
                    nc.vector.tensor_copy(h2c[:, c * CH:(c + 1) * CH], got[:, :, 1]).then_inc(taken, 1)
                dve.wait_ge(averaged_h, 1)
                nc.vector.tensor_copy(mean_h[:, :], pM[:, 0:D]).then_inc(mean_out, 1)
                dve.wait_ge(mean_out, 2)
                dve.wait_ge(taken, NCH)

            @block.gpsimd
            def _(pool):
                pool.dma_start(aw[:, :], a2).then_inc(a_in, 16)
                pool.wait_ge(a_in, 16)
                nc.gpsimd.tensor_scalar(a1w[:, :], ones[:, :], aw[:, 0:1], None, ALU.mult).then_inc(a_wide, 1)
                nc.gpsimd.memset(nth[:, :], 1.0 / N).then_inc(a_wide, 2)

            normalise(nc, ph, block, x, h, on_pe, on_act, on_dve)


def general_maxima(nc, ident, ones, adjG, h1c, h2c, mb):
    with Phase(nc, "mx") as ph:
        adj = ph.sb("adj", [P, 2, WB], I32)
        off = ph.sb("off", [P, 2, WB])
        best = ph.sb("best", [P, WB])
        top = ph.sb("top", [P, NT])
        s = ph.sb("s", [P, NT])
        m = ph.sb("m", [P, NT])
        diag = ph.sb("diag", [P, 2, P])
        pR = ph.ps("pR", [P, TB, 128])
        pD = ph.ps("pD", [P, 2, 512])
        adj_in = [ph.sem(f"adj_in{b}") for b in range(2)]
        adj_used = [ph.sem(f"adj_used{b}") for b in range(2)]
        best_set, turned, topped, m_ready = (
            ph.sem(n) for n in ("best_set", "turned", "topped", "m_ready"))
        diag_ready = [ph.sem(f"diag_ready{b}") for b in range(2)]
        diag_used = [ph.sem(f"diag_used{b}") for b in range(2)]
        row_out = [ph.sem(f"row_out{b}") for b in range(2)]
        with nc.Block() as block:
            @block.sync
            def _(sp):
                for b in range(2):
                    sp.sem_inc(adj_used[b], 1)
                with sp.Fori(0, NB) as i:
                    with sp.Fori(0, NG) as g:
                        for j in range(GT):
                            q, b = g * 2 + j // 2, j % 2
                            sp.wait_ge(adj_used[b], i * NPAIR + q + 1)
                            sp.dma_start(adj[:, b, :], adjG[bass.ds(i * NG + g, 1), :, j, :].squeeze(0)
                                         ).then_inc(adj_in[b], 16)

            @block.vector
            def _(dve):
                dve.sem_inc(turned, 1)
                for b in range(2):
                    dve.sem_inc(diag_used[b], 1)
                with dve.Fori(0, NB) as i:
                    dve.wait_ge(turned, i + 1)
                    nc.vector.memset(best[:, :], LOW).then_inc(best_set, 1)
                    with dve.Fori(0, NPAIR) as q:
                        for b in range(2):
                            dve.wait_ge(adj_in[b], (i * NPAIR + q + 1) * 16)
                            nc.vector.tensor_scalar(off[:, b, :], adj[:, b, :], 0.0, LOW, ALU.is_le,
                                                    ALU.mult).then_inc(adj_used[b], 1)
                            dve.wait_ge(adj_used[b], i * NPAIR + q + 2)
                            dve.wait_ge(best_set, i * (2 * NPAIR + 1) + q * 2 + b + 1)
                            nc.vector.scalar_tensor_tensor(
                                out=best[:, :], in0=off[:, b, :], scalar=h2c[:, bass.ds(q * 2 + b, 1)],
                                in1=best[:, :], op0=ALU.add, op1=ALU.max).then_inc(best_set, 1)
                    dve.wait_ge(turned, i + 2)
                    nc.vector.reduce_max(top[:, bass.ds(i * TB, TB)], pR[:, :, :], AX).then_inc(topped, 1)
                dve.wait_ge(topped, NB + 1)
                nc.vector.tensor_tensor(s[:, :], h1c[:, :], top[:, :], ALU.add).then_inc(m_ready, 1)
                dve.wait_ge(m_ready, 1)
                nc.vector.scalar_tensor_tensor(out=m[:, :], in0=s[:, :], scalar=SLOPE, in1=s[:, :],
                                               op0=ALU.mult, op1=ALU.max).then_inc(m_ready, 1)
                dve.wait_ge(m_ready, 2)
                with dve.Fori(0, NPAIR) as q:
                    for b in range(2):
                        dve.wait_ge(diag_used[b], q + 1)
                        nc.vector.tensor_scalar(diag[:, b, :], ident[:, :], m[:, bass.ds(q * 2 + b, 1)], None,
                                                ALU.mult).then_inc(diag_ready[b], 1)

            @block.tensor
            def _(pe):
                pe.sem_inc(topped, 1)
                for b in range(2):
                    pe.sem_inc(row_out[b], 1)
                with pe.Fori(0, NB) as i:
                    pe.wait_ge(best_set, (i + 1) * (2 * NPAIR + 1))
                    pe.wait_ge(topped, i + 1)
                    for t in range(TB):
                        last = nc.tensor.transpose(pR[:, t, :], best[:, t * P:(t + 1) * P], ident[:, :])
                    last.then_inc(turned, 1)
                with pe.Fori(0, NPAIR) as q:
                    for b in range(2):
                        pe.wait_ge(diag_ready[b], q + 1)
                        pe.wait_ge(row_out[b], q + 1)
                        nc.tensor.matmul(pD[:, b, 0:P], ones[:, :], diag[:, b, :], start=True,
                                         stop=True).then_inc(diag_used[b], 1)

            @block.scalar
            def _(act):
                with act.Fori(0, NPAIR) as q:
                    for b in range(2):
                        act.wait_ge(diag_used[b], q + 2)
                        nc.scalar.activation(mb[:, bass.ds((q * 2 + b) * P, P)], pD[:, b, 0:P],
                                             ACT.Copy).then_inc(row_out[b], 1)


def general_attention(nc, x, adjG, h, h2c, h1b, mb, mean_h, x1):
    with Phase(nc, "at") as ph:
        adj = ph.sb("adj", [P, 2, WB], I32)
        z = ph.sb("z", [P, 2, WB])
        e = ph.sb("e", [P, 2, WB])
        dd = ph.sb("dd", [P, 2, WB])
        below = ph.sb("below", [P, 2, WB])
        w = ph.sb("w", [P, 2, WB])
        pw = ph.sb("pw", [P, 2, WB])
        acc = ph.ps("acc", [P, TB, 512])
        num = ph.sb("num", [P, TB, D1])
        alone, den, inv = (ph.sb(n, [P, TB]) for n in ("alone", "den", "inv"))
        part = ph.sb("part", [P, TB, D])
        mh = ph.sb("mh", [P, TB, D])
        xin = ph.sb("xin", [P, TB, D])
        adj_in = [ph.sem(f"adj_in{b}") for b in range(2)]
        w_ready = [ph.sem(f"w_ready{b}") for b in range(2)]
        d_ready = [ph.sem(f"d_ready{b}") for b in range(2)]
        b_ready = [ph.sem(f"b_ready{b}") for b in range(2)]
        p_ready = [ph.sem(f"p_ready{b}") for b in range(2)]
        p_used = [ph.sem(f"p_used{b}") for b in range(2)]
        z_ready, e_ready, drained, fin, x_in, x_out = (
            ph.sem(n) for n in ("z_ready", "e_ready", "drained", "fin", "x_in", "x_out"))
        FIN = 7
        xt = x.rearrange("(i t p) d -> i p t d", p=P, t=TB)
        x1t = x1.rearrange("(i t p) d -> i p t d", p=P, t=TB)
        with nc.Block() as block:
            @block.sync
            def _(sp):
                for b in range(2):
                    sp.sem_inc(p_ready[b], 1)
                with sp.Fori(0, NB) as i:
                    with sp.Fori(0, NG) as g:
                        for j in range(GT):
                            q, b = g * 2 + j // 2, j % 2
                            sp.wait_ge(p_ready[b], i * NPAIR + q + 1)
                            sp.dma_start(adj[:, b, :], adjG[bass.ds(i * NG + g, 1), :, j, :].squeeze(0)
                                         ).then_inc(adj_in[b], 16)

            @block.scalar
            def _(act):
                act.sem_inc(fin, 1)
                with act.Fori(0, NB) as i:
                    act.wait_ge(fin, i * FIN + 1)
                    act.dma_start(xin[:, :, :], xt[bass.ds(i, 1), :, :, :].squeeze(0)).then_inc(x_in, 16)
                    with act.Fori(0, NPAIR) as q:
                        for b in range(2):
                            n = i * NPAIR + q
                            act.wait_ge(d_ready[b], n + 1)
                            nc.scalar.activation(below[:, b, :], dd[:, b, :], ACT.Relu,
                                                 scale=-1.0).then_inc(b_ready[b], 1)
                            act.wait_ge(b_ready[b], n + 2)
                            act.wait_ge(p_ready[b], n + 1)
                            nc.scalar.activation(w[:, b, :], below[:, b, :], ACT.Exp,
                                                 scale=-1.0).then_inc(w_ready[b], 1)
                    act.wait_ge(fin, (i + 1) * FIN + 1)
                    act.dma_start(x1t[bass.ds(i, 1), :, :, :].squeeze(0), part[:, :, :]).then_inc(x_out, 16)
                    act.wait_ge(x_out, (i + 1) * 16)

            @block.vector
            def _(dve):
                for b in range(2):
                    dve.sem_inc(b_ready[b], 1)
                    dve.sem_inc(p_used[b], 1)
                with dve.Fori(0, NB) as i:
                    with dve.Fori(0, NPAIR) as q:
                        for b in range(2):
                            n = i * NPAIR + q
                            cols = bass.ds(i * WB, WB)
                            nc.vector.tensor_scalar(z[:, b, :], h1b[:, cols], h2c[:, bass.ds(q * 2 + b, 1)], None,
                                                    ALU.add).then_inc(z_ready, 1)
                            dve.wait_ge(z_ready, n * 2 + b + 1)
                            nc.vector.scalar_tensor_tensor(out=e[:, b, :], in0=z[:, b, :], scalar=SLOPE,
                                                           in1=z[:, b, :], op0=ALU.mult,
                                                           op1=ALU.max).then_inc(e_ready, 1)
                            dve.wait_ge(e_ready, n * 2 + b + 1)
                            dve.wait_ge(b_ready[b], n + 1)
                            nc.vector.tensor_tensor(dd[:, b, :], e[:, b, :], mb[:, cols],
                                                    ALU.subtract).then_inc(d_ready[b], 1)
                        for b in range(2):
                            n = i * NPAIR + q
                            dve.wait_ge(w_ready[b], n + 1)
                            dve.wait_ge(adj_in[b], (n + 1) * 16)
                            dve.wait_ge(p_used[b], n + 1)
                            nc.vector.scalar_tensor_tensor(out=pw[:, b, :], in0=adj[:, b, :], scalar=0.0,
                                                           in1=w[:, b, :], op0=ALU.is_gt,
                                                           op1=ALU.mult).then_inc(p_ready[b], 1)
                    dve.wait_ge(p_used[1], (i + 1) * NPAIR + 1)
                    nc.vector.tensor_copy(num[:, :, :], acc[:, :, 0:D1]).then_inc(drained, 1)
                    dve.wait_ge(drained, i + 2)
                    nc.vector.tensor_scalar(alone[:, :], num[:, :, D], 0.0, None, ALU.is_equal).then_inc(fin, 1)
                    dve.wait_ge(fin, i * FIN + 2)
                    nc.vector.tensor_tensor(den[:, :], num[:, :, D], alone[:, :], ALU.add).then_inc(fin, 1)
                    dve.wait_ge(fin, i * FIN + 3)
                    nc.vector.reciprocal(inv[:, :], den[:, :]).then_inc(fin, 1)
                    dve.wait_ge(fin, i * FIN + 4)
                    dve.wait_ge(x_in, (i + 1) * 16)
                    nc.vector.tensor_tensor(part[:, :, :], num[:, :, 0:D],
                                            inv[:, :].unsqueeze(2).to_broadcast([P, TB, D]), ALU.mult).then_inc(fin, 1)
                    nc.vector.tensor_tensor(mh[:, :, :], alone[:, :].unsqueeze(2).to_broadcast([P, TB, D]),
                                            mean_h[:, :].unsqueeze(1).to_broadcast([P, TB, D]),
                                            ALU.mult).then_inc(fin, 1)
                    dve.wait_ge(fin, i * FIN + 6)
                    nc.vector.tensor_tensor(part[:, :, :], part[:, :, :], mh[:, :, :], ALU.add).then_inc(fin, 1)
                    dve.wait_ge(fin, i * FIN + 7)
                    nc.vector.tensor_tensor(part[:, :, :], part[:, :, :], xin[:, :, :], ALU.add).then_inc(fin, 1)

            @block.tensor
            def _(pe):
                def step(i, q, b, first):
                    pe.wait_ge(p_ready[b], i * NPAIR + q + 2)
                    for t in range(TB):
                        last = nc.tensor.matmul(acc[:, t, 0:D1], pw[:, b, t * P:(t + 1) * P],
                                                h[:, bass.ds(q * 2 + b, 1), :].squeeze(1), start=first, stop=False,
                                                skip_group_check=True)
                    last.then_inc(p_used[b], 1)

                pe.sem_inc(drained, 1)
                with pe.Fori(0, NB) as i:
                    pe.wait_ge(drained, i + 1)
                    step(i, 0, 0, True)
                    step(i, 0, 1, False)
                    with pe.Fori(1, NPAIR) as q:
                        for b in range(2):
                            step(i, q, b, False)


def values_phase(nc, ident, x1, ws, h, vw):
    K = len(ws)
    with Phase(nc, "va") as ph:
        wt = ph.sb("wt", [D, K, D])
        hT = ph.sb("hT", [D, 2, CH * P])
        pT = ph.ps("pT", [D, 2, CH * P])
        pV = ph.ps("pV", [P, CH, 512])
        w_in, turned, hT_ready, projected, taken = (
            ph.sem(n) for n in ("w_in", "turned", "hT_ready", "projected", "taken"))
        with nc.Block() as block:
            def on_pe(pe, normed):
                pe.wait_ge(w_in, 16 * K)
                for k in range(NCH + 1):
                    if k < NCH:
                        pe.wait_ge(normed, k * CH // LC + 1)
                        if k >= 2:
                            pe.wait_ge(hT_ready, k - 1)
                        for t in range(CH):
                            last = nc.tensor.transpose(pT[:, k % 2, t * P:(t + 1) * P],
                                                       h[:, k * CH + t, 0:D], ident[:, :])
                        last.then_inc(turned, 1)
                    if k >= 1:
                        c = k - 1
                        pe.wait_ge(hT_ready, c + 1)
                        for t in range(CH):
                            if c >= 1:
                                pe.wait_ge(taken, (c - 1) * CH + t + 1)
                            nc.tensor.matmul(pV[:, t, 0:K * D], hT[:, c % 2, t * P:(t + 1) * P],
                                             wt[:, :, :].rearrange("p k d -> p (k d)"),
                                             start=True, stop=True).then_inc(projected, 1)

            def on_act(act, normed):
                for k in range(NCH):
                    act.wait_ge(turned, k + 1)
                    if k >= 2:
                        act.wait_ge(projected, (k - 1) * CH)
                    nc.scalar.activation(hT[:, k % 2, :], pT[:, k % 2, :], ACT.Copy).then_inc(hT_ready, 1)

            def on_dve(dve, normed):
                for n in range(NT):
                    dve.wait_ge(projected, n + 1)
                    nc.vector.tensor_copy(vw[:, n, :, :].rearrange("p k d -> p (k d)"),
                                          pV[:, n % CH, 0:K * D]).then_inc(taken, 1)
                dve.wait_ge(taken, NT)

            @block.gpsimd
            def _(pool):
                for k in range(K):
                    pool.dma_start(wt[:, k, :], ws[k]).then_inc(w_in, 16)

            normalise(nc, ph, block, x1, h, on_pe, on_act, on_dve)


def general_kinds(nc, adjG, vw, x1, bias, out):
    K = 3
    with Phase(nc, "ki") as ph:
        adj = ph.sb("adj", [P, 2, WB], I32)
        mask = ph.sb("mask", [P, 2, K, WB])
        acc = ph.ps("acc", [P, TB, 512])
        res = ph.sb("res", [P, TB, D])
        xin = ph.sb("xin", [P, TB, D])
        brow = ph.sb("brow", [P, D])
        adj_in = [ph.sem(f"adj_in{b}") for b in range(2)]
        m_ready = [ph.sem(f"m_ready{b}") for b in range(2)]
        m_used = [ph.sem(f"m_used{b}") for b in range(2)]
        b_in, fin, x_in, x_out = (ph.sem(n) for n in ("b_in", "fin", "x_in", "x_out"))
        FIN = 2
        x1t = x1.rearrange("(i t p) d -> i p t d", p=P, t=TB)
        ot = out.rearrange("(i t p) d -> i p t d", p=P, t=TB)
        with nc.Block() as block:
            @block.sync
            def _(sp):
                for b in range(2):
                    sp.sem_inc(m_ready[b], 1)
                sp.dma_start(brow[:, :], bias.partition_broadcast(P)).then_inc(b_in, 16)
                with sp.Fori(0, NB) as i:
                    with sp.Fori(0, NG) as g:
                        for j in range(GT):
                            q, b = g * 2 + j // 2, j % 2
                            sp.wait_ge(m_ready[b], (i * NPAIR + q) * K + 1)
                            sp.dma_start(adj[:, b, :], adjG[bass.ds(i * NG + g, 1), :, j, :].squeeze(0)
                                         ).then_inc(adj_in[b], 16)

            @block.scalar
            def _(act):
                act.sem_inc(fin, 1)
                with act.Fori(0, NB) as i:
                    act.wait_ge(fin, i * FIN + 1)
                    act.dma_start(xin[:, :, :], x1t[bass.ds(i, 1), :, :, :].squeeze(0)).then_inc(x_in, 16)
                    act.wait_ge(fin, (i + 1) * FIN + 1)
                    act.dma_start(ot[bass.ds(i, 1), :, :, :].squeeze(0), res[:, :, :]).then_inc(x_out, 16)
                    act.wait_ge(x_out, (i + 1) * 16)

            @block.vector
            def _(dve):
                for b in range(2):
                    dve.sem_inc(m_used[b], 1)
                dve.wait_ge(b_in, 16)
                with dve.Fori(0, NB) as i:
                    with dve.Fori(0, NPAIR) as q:
                        for b in range(2):
                            n = i * NPAIR + q
                            dve.wait_ge(adj_in[b], (n + 1) * 16)
                            dve.wait_ge(m_used[b], n + 1)
                            for k in range(K):
                                nc.vector.tensor_scalar(mask[:, b, k, :], adj[:, b, :], float(k + 1), None,
                                                        ALU.is_equal).then_inc(m_ready[b], 1)
                    dve.wait_ge(m_used[1], (i + 1) * NPAIR + 1)
                    dve.wait_ge(x_in, (i + 1) * 16)
                    nc.vector.tensor_tensor(res[:, :, :], acc[:, :, 0:D], xin[:, :, :], ALU.add).then_inc(fin, 1)
                    dve.wait_ge(fin, i * FIN + 2)
                    nc.vector.tensor_tensor(res[:, :, :], res[:, :, :],
                                            brow[:, :].unsqueeze(1).to_broadcast([P, TB, D]),
                                            ALU.add).then_inc(fin, 1)

            @block.tensor
            def _(pe):
                def step(i, q, b, first):
                    pe.wait_ge(m_ready[b], (i * NPAIR + q + 1) * K + 1)
                    for t in range(TB):
                        for k in range(K):
                            last = nc.tensor.matmul(acc[:, t, 0:D], mask[:, b, k, t * P:(t + 1) * P],
                                                    vw[:, bass.ds(q * 2 + b, 1), k, :].squeeze(1),
                                                    start=(first and k == 0), stop=False, skip_group_check=True)
                    last.then_inc(m_used[b], 1)

                with pe.Fori(0, NB) as i:
                    pe.wait_ge(fin, i * FIN + 1)
                    step(i, 0, 0, True)
                    step(i, 0, 1, False)
                    with pe.Fori(1, NPAIR) as q:
                        for b in range(2):
                            step(i, q, b, False)


def general_layers(nc, ident, ones, x, adjG, a2, ws, bias, x1, out):
    with Phase(nc, "ge") as ph:
        with Phase(nc, "g0") as p0:
            h = p0.sb("h", [P, NT, D1])
            h1c, h2c = p0.sb("h1c", [P, NT]), p0.sb("h2c", [P, NT])
            mean_h = p0.sb("mean_h", [P, D])
            h1b = p0.sb("h1b", [P, N])
            scores_phase(nc, "gs", ident, ones, x, a2, h, h1c, h2c, h1b, mean_h)
            mb = p0.sb("mb", [P, N])
            general_maxima(nc, ident, ones, adjG, h1c, h2c, mb)
            general_attention(nc, x, adjG, h, h2c, h1b, mb, mean_h, x1)
        with Phase(nc, "g1") as p1:
            vw = p1.sb("vw", [P, NT, 3, D])
            with Phase(nc, "g2") as p2:
                h = p2.sb("h", [P, NT, D])
                values_phase(nc, ident, x1, ws, h, vw)
            general_kinds(nc, adjG, vw, x1, bias, out)


def factors_phase(nc, h, h1c, h2c, ef, nh2, e1, f1, spread_ok):
    with Phase(nc, "fa") as ph:
        ends = ph.sb("ends", [P, 2])
        top = ph.sb("top", [P, 2])
        nc0, nc1, width = ph.sb("nc0", [P, 1]), ph.sb("nc1", [P, 1]), ph.sb("width", [P, 1])
        z, zs, lo, hi = (ph.sb(n, [P, NT]) for n in ("z", "zs", "lo", "hi"))
        src = ph.sb("src", [P, 2, NT])
        srcs = ph.sb("srcs", [P, 2, NT])
        ended, topped, bound, made, exped, scaled, upper, lower = (
            ph.sem(n) for n in ("ended", "topped", "bound", "made", "exped", "scaled", "upper", "lower"))
        with nc.Block() as block:
            @block.gpsimd
            def _(pool):
                pool.wait_ge(ended, 3)
                nc.gpsimd.partition_all_reduce(top[:, :], ends[:, :], P, bass.bass_isa.ReduceOp.max
                                               ).then_inc(topped, 1)

            @block.vector
            def _(dve):
                nc.vector.tensor_scalar(nh2[:, :], h2c[:, :], -1.0, None, ALU.mult).then_inc(ended, 1)
                nc.vector.reduce_max(ends[:, 0:1], h2c[:, :], AX).then_inc(ended, 1)
                dve.wait_ge(ended, 2)
                nc.vector.reduce_max(ends[:, 1:2], nh2[:, :], AX).then_inc(ended, 1)
                dve.wait_ge(topped, 1)
                nc.vector.tensor_scalar(nc0[:, :], top[:, 0:1], -1.0, None, ALU.mult).then_inc(bound, 1)
                nc.vector.tensor_scalar(nc1[:, :], top[:, 0:1], -SLOPE, None, ALU.mult).then_inc(bound, 1)
                nc.vector.tensor_tensor(width[:, :], top[:, 0:1], top[:, 1:2], ALU.add).then_inc(made, 1)
                nc.vector.tensor_scalar(z[:, :], h1c[:, :], top[:, 0:1], 1.0 - SLOPE, ALU.add,
                                        ALU.mult).then_inc(made, 1)
                dve.wait_ge(made, 2)
                nc.vector.tensor_scalar(spread_ok[:, :], width[:, :], SPREAD, None, ALU.is_le).then_inc(made, 1)
                nc.vector.tensor_scalar(lo[:, :], z[:, :], 0.0, None, ALU.min).then_inc(made, 1)
                nc.vector.tensor_scalar(hi[:, :], z[:, :], 0.0, None, ALU.max).then_inc(made, 1)
                dve.wait_ge(made, 5)
                dve.wait_ge(exped, 2)
                nc.vector.tensor_scalar(srcs[:, :, :], src[:, :, :], SCALE, None, ALU.mult).then_inc(scaled, 1)
                dve.wait_ge(scaled, 1)
                with dve.Fori(0, NT) as t:
                    for k in range(2):
                        dve.wait_ge(upper, t * 2 + k + 1)
                        nc.vector.scalar_tensor_tensor(
                            out=ef[:, bass.ds(t, 1), k, 1, :].squeeze(1), in0=h[:, bass.ds(t, 1), :].squeeze(1),
                            scalar=srcs[:, k, bass.ds(t, 1)], in1=ef[:, bass.ds(t, 1), k, 0, :].squeeze(1),
                            op0=ALU.mult, op1=ALU.subtract).then_inc(lower, 1)
                dve.wait_ge(lower, 2 * NT)

            @block.scalar
            def _(act):
                act.wait_ge(bound, 2)
                nc.scalar.activation(src[:, 0, :], h2c[:, :], ACT.Exp, bias=nc0[:, 0:1]).then_inc(exped, 1)
                nc.scalar.activation(src[:, 1, :], h2c[:, :], ACT.Exp, bias=nc1[:, 0:1], scale=SLOPE
                                     ).then_inc(exped, 1)
                act.wait_ge(made, 5)
                nc.scalar.activation(e1[:, :], lo[:, :], ACT.Exp).then_inc(exped, 1)
                nc.scalar.activation(f1[:, :], hi[:, :], ACT.Exp, scale=-1.0).then_inc(exped, 1)
                act.wait_ge(exped, 4)
                act.wait_ge(scaled, 1)
                with act.Fori(0, NT) as t:
                    for k in range(2):
                        nc.scalar.activation(ef[:, bass.ds(t, 1), k, 0, :].squeeze(1),
                                             h[:, bass.ds(t, 1), :].squeeze(1), ACT.Copy,
                                             scale=srcs[:, k, bass.ds(t, 1)]).then_inc(upper, 1)


def fast_attention(nc, x, adjG, ef, nh2, e1, f1, h1b, mean_h, a8d, x1):
    with Phase(nc, "fl") as ph:
        adj = ph.sb("adj", [P, 2, GW], I32)
        a16 = ph.sb("a16", [P, 2, GW], F16)
        a8 = ph.sb("a8", [P, 2, GW], F8)
        above = ph.sb("above", [P, 2, GW], F16)
        under = ph.sb("under", [P, 2, GW], F16)
        num = ph.sb("num", [P, TB, D1])
        tmp = ph.sb("tmp", [P, TB, D1])
        xin = ph.sb("xin", [P, TB, D])
        alone, den, inv = (ph.sb(n, [P, TB]) for n in ("alone", "den", "inv"))
        acc = ph.ps("acc", [P, TB, 512])

        def pair_of(name):
            return [ph.sem(f"{name}{b}") for b in range(2)]

        adj_in, a16_ready, a8_ready, a8_out, above_ready, under_ready, used = (
            pair_of(n) for n in ("adj_in", "a16_ready", "a8_ready", "a8_out", "above_ready", "under_ready", "used"))
        below_out, drained, fin, x_in, x_out, x_go, act_step = (
            ph.sem(n) for n in ("below_out", "drained", "fin", "x_in", "x_out", "x_go", "act_step"))
        FIN = 4 + TB + 1
        PB = NG // 2
        xt = x.rearrange("(i t p) d -> i p t d", p=P, t=TB)
        x1t = x1.rearrange("(i t p) d -> i p t d", p=P, t=TB)
        with nc.Block() as block:
            @block.sync
            def _(sp):
                def load(m, b):
                    sp.dma_start(adj[:, b, :], adjG[bass.ds(m * 2 + b, 1), :, :, :].squeeze(0)
                                 .rearrange("p t w -> p (t w)")).then_inc(adj_in[b], 16)

                def store(m, b):
                    sp.dma_start(a8d[bass.ds(m * 2 + b, 1), :, :].squeeze(0), a8[:, b, :].bitcast(U8)
                                 ).then_inc(a8_out[b], 16)

                for b in range(2):
                    load(0, b)
                with sp.Fori(1, MP) as m:
                    for b in range(2):
                        sp.wait_ge(a16_ready[b], m)
                        load(m, b)
                        sp.wait_ge(a8_ready[b], m)
                        store(m - 1, b)
                for b in range(2):
                    sp.wait_ge(a8_ready[b], MP)
                    store(MP - 1, b)
                for b in range(2):
                    sp.wait_ge(a8_out[b], MP * 16)

            @block.scalar
            def _(act):
                def convert(m, b, first):
                    act.wait_ge(adj_in[b], (m + 1) * 16)
                    if not first:
                        act.wait_ge(under_ready[b], m)
                    nc.scalar.activation(a16[:, b, :], adj[:, b, :], ACT.Copy).then_inc(a16_ready[b], 1)
                    act.wait_ge(a16_ready[b], m + 1)
                    if not first:
                        act.wait_ge(a8_out[b], m * 16)
                    act.sem_inc(act_step, 1)
                    nc.scalar.activation(a8[:, b, :], a16[:, b, :], ACT.Copy, saturate=False
                                         ).then_inc(a8_ready[b], 1)

                for b in range(2):
                    convert(0, b, True)
                with act.Fori(1, MP) as m:
                    for b in range(2):
                        convert(m, b, False)

            @block.gpsimd
            def _(pool):
                pool.sem_inc(fin, 1)
                with pool.Fori(0, NB) as i:
                    pool.wait_ge(fin, i * FIN + 1)
                    pool.sem_inc(x_go, 1)
                    pool.dma_start(xin[:, :, :], xt[bass.ds(i, 1), :, :, :].squeeze(0)).then_inc(x_in, 16)
                    pool.wait_ge(fin, (i + 1) * FIN + 1)
                    pool.sem_inc(x_go, 1)
                    pool.dma_start(x1t[bass.ds(i, 1), :, :, :].squeeze(0), xin[:, :, :]).then_inc(x_out, 16)
                    pool.wait_ge(x_out, (i + 1) * 16)
                    pool.sem_inc(x_go, 1)

            @block.vector
            def _(dve):
                def split(i, q, b, first):
                    m = i * PB + q
                    dve.wait_ge(a16_ready[b], m + 1)
                    if not first:
                        dve.wait_ge(used[b], m)
                    for j in range(GT):
                        cols = slice(j * WB, (j + 1) * WB)
                        nc.vector.scalar_tensor_tensor(
                            out=above[:, b, cols], in0=h1b[:, bass.ds(i * WB, WB)],
                            scalar=nh2[:, bass.ds((q * 2 + b) * GT + j, 1)], in1=a16[:, b, cols],
                            op0=ALU.is_gt, op1=ALU.mult).then_inc(above_ready[b], 1)
                    dve.wait_ge(above_ready[b], (m + 1) * GT)
                    nc.vector.tensor_tensor(under[:, b, :], a16[:, b, :], above[:, b, :],
                                            ALU.subtract).then_inc(under_ready[b], 1)

                def finish(i):
                    dve.wait_ge(used[1], (i + 1) * PB)
                    for t in range(TB + 1):
                        if t < TB:
                            nc.vector.tensor_scalar(tmp[:, t, :], acc[:, t, D1:2 * D1], f1[:, bass.ds(i * TB + t, 1)],
                                                    None, ALU.mult).then_inc(below_out, 1)
                        if t >= 1:
                            dve.wait_ge(below_out, i * TB + t)
                            nc.vector.scalar_tensor_tensor(
                                out=num[:, t - 1, :], in0=acc[:, t - 1, 0:D1], scalar=e1[:, bass.ds(i * TB + t - 1, 1)],
                                in1=tmp[:, t - 1, :], op0=ALU.mult, op1=ALU.add).then_inc(drained, 1)
                    dve.wait_ge(drained, (i + 1) * TB)
                    nc.vector.tensor_scalar(alone[:, :], num[:, :, D], 0.0, None, ALU.is_equal).then_inc(fin, 1)
                    dve.wait_ge(fin, i * FIN + 2)
                    nc.vector.tensor_tensor(den[:, :], num[:, :, D], alone[:, :], ALU.add).then_inc(fin, 1)
                    dve.wait_ge(fin, i * FIN + 3)
                    nc.vector.reciprocal(inv[:, :], den[:, :]).then_inc(fin, 1)
                    dve.wait_ge(fin, i * FIN + 4)
                    nc.vector.tensor_tensor(tmp[:, :, 0:D], num[:, :, 0:D],
                                            inv[:, :].unsqueeze(2).to_broadcast([P, TB, D]), ALU.mult).then_inc(fin, 1)
                    dve.wait_ge(fin, i * FIN + 5)
                    for t in range(TB):
                        nc.vector.scalar_tensor_tensor(out=num[:, t, 0:D], in0=mean_h[:, :], scalar=alone[:, t:t + 1],
                                                       in1=tmp[:, t, 0:D], op0=ALU.mult, op1=ALU.add).then_inc(fin, 1)
                    dve.wait_ge(fin, i * FIN + 5 + TB)
                    dve.wait_ge(x_in, (i + 1) * 16)
                    nc.vector.tensor_tensor(xin[:, :, :], num[:, :, 0:D], xin[:, :, :], ALU.add).then_inc(fin, 1)

                def rest(i):
                    with dve.Fori(1, PB) as q:
                        for b in range(2):
                            split(i, q, b, False)

                for b in range(2):
                    split(0, 0, b, True)
                with dve.Fori(0, NB - 1) as i:
                    rest(i)
                    for b in range(2):
                        split(i + 1, 0, b, False)
                    finish(i)
                rest(NB - 1)
                finish(NB - 1)

            @block.tensor
            def _(pe):
                def products(i, q, b, start, wait_banks):
                    pe.wait_ge(under_ready[b], i * PB + q + 1)
                    for j in range(GT):
                        for t in range(TB):
                            if wait_banks and j == 0:
                                pe.wait_ge(drained, i * TB + t - TB + 1)
                            cols = slice(j * WB + t * P, j * WB + (t + 1) * P)
                            for k, mask in enumerate((above, under)):
                                for part in range(2):
                                    last = nc.tensor.matmul(
                                        acc[:, t, k * D1:(k + 1) * D1], mask[:, b, cols],
                                        ef[:, bass.ds((q * 2 + b) * GT + j, 1), k, part, :].squeeze(1),
                                        start=(start and j == 0 and k == 0 and part == 0), stop=False,
                                        skip_group_check=True)
                    last.then_inc(used[b], 1)

                def block_of(i, wait_banks):
                    products(i, 0, 0, True, wait_banks)
                    products(i, 0, 1, False, False)
                    with pe.Fori(1, PB) as q:
                        for b in range(2):
                            products(i, q, b, False, False)

                block_of(0, False)
                with pe.Fori(1, NB) as i:
                    block_of(i, True)


def fast_values(nc, ident, x1, w1, vw, unscale):
    with Phase(nc, "fv") as ph:
        h = ph.sb("h", [P, NT, D])
        wt = ph.sb("wt", [D, D])
        wneg = ph.sb("wneg", [D, D])
        ends, top = ph.sb("ends", [P, 2]), ph.sb("top", [P, 2])
        big, power, inverse, scale = (ph.sb(n, [P, 1]) for n in ("big", "power", "inverse", "scale"))
        hT = ph.sb("hT", [D, 2, CH * P])
        pT = ph.ps("pT", [D, 2, CH * P])
        pV = ph.ps("pV", [P, 2, CH * P])
        w_in, ended, topped, scaled, turned, hT_ready, projected, upper, lower = (
            ph.sem(n) for n in ("w_in", "ended", "topped", "scaled", "turned", "hT_ready", "projected", "upper",
                                "lower"))
        with nc.Block() as block:
            @block.gpsimd
            def _(pool):
                pool.dma_start(wt[:, :], w1).then_inc(w_in, 16)
                pool.wait_ge(ended, 3)
                nc.gpsimd.partition_all_reduce(top[:, :], ends[:, :], P, bass.bass_isa.ReduceOp.max
                                               ).then_inc(topped, 1)

            def on_pe(pe, normed):
                pe.wait_ge(w_in, 16)
                for k in range(NCH + 1):
                    if k < NCH:
                        pe.wait_ge(normed, k * CH // LC + 1)
                        if k >= 2:
                            pe.wait_ge(hT_ready, k - 1)
                        for t in range(CH):
                            last = nc.tensor.transpose(pT[:, k % 2, t * P:(t + 1) * P],
                                                       h[:, k * CH + t, 0:D], ident[:, :])
                        last.then_inc(turned, 1)
                    if k >= 1:
                        c = k - 1
                        pe.wait_ge(hT_ready, c + 1)
                        if c >= 2:
                            pe.wait_ge(lower, c - 1)
                        for t in range(CH):
                            last = nc.tensor.matmul(pV[:, c % 2, t * P:(t + 1) * P],
                                                    hT[:, c % 2, t * P:(t + 1) * P], wt[:, :],
                                                    start=True, stop=True)
                        last.then_inc(projected, 1)

            def on_act(act, normed):
                act.wait_ge(scaled, 5)
                for k in range(NCH + 1):
                    if k < NCH:
                        act.wait_ge(turned, k + 1)
                        if k >= 2:
                            act.wait_ge(projected, k - 1)
                        nc.scalar.activation(hT[:, k % 2, :], pT[:, k % 2, :], ACT.Copy).then_inc(hT_ready, 1)
                    if k >= 1:
                        c = k - 1
                        act.wait_ge(projected, c + 1)
                        nc.scalar.activation(vw[:, c * CH:(c + 1) * CH, 0, :],
                                             pV[:, c % 2, :].rearrange("p (t d) -> p t d", d=D), ACT.Copy,
                                             scale=scale[:, 0:1]).then_inc(upper, 1)

            def on_dve(dve, normed):
                dve.wait_ge(w_in, 16)
                nc.vector.reduce_max(ends[:, 0:1], wt[:, :], AX).then_inc(ended, 1)
                nc.vector.tensor_scalar(wneg[:, :], wt[:, :], -1.0, None, ALU.mult).then_inc(ended, 1)
                dve.wait_ge(ended, 2)
                nc.vector.reduce_max(ends[:, 1:2], wneg[:, :], AX).then_inc(ended, 1)
                dve.wait_ge(topped, 1)
                nc.vector.tensor_scalar(big[:, :], top[:, 0:1], top[:, 1:2], 1e-30, ALU.max,
                                        ALU.max).then_inc(scaled, 1)
                dve.wait_ge(scaled, 1)
                nc.vector.tensor_scalar(power[:, :].bitcast(I32), big[:, :].bitcast(I32), 0x7F800000, None,
                                        ALU.bitwise_and).then_inc(scaled, 1)
                dve.wait_ge(scaled, 2)
                nc.vector.reciprocal(inverse[:, :], power[:, :]).then_inc(scaled, 1)
                nc.vector.tensor_scalar(unscale[:, :], power[:, :], 1.0 / D, None, ALU.mult).then_inc(scaled, 1)
                dve.wait_ge(scaled, 4)
                nc.vector.tensor_scalar(scale[:, :], inverse[:, :], float(D), None, ALU.mult).then_inc(scaled, 1)
                dve.wait_ge(scaled, 5)
                for c in range(NCH):
                    dve.wait_ge(upper, c + 1)
                    nc.vector.scalar_tensor_tensor(
                        out=vw[:, c * CH:(c + 1) * CH, 1, :], in0=pV[:, c % 2, :].rearrange("p (t d) -> p t d", d=D),
                        scalar=scale[:, 0:1], in1=vw[:, c * CH:(c + 1) * CH, 0, :], op0=ALU.mult,
                        op1=ALU.subtract).then_inc(lower, 1)
                dve.wait_ge(lower, NCH)

            normalise(nc, ph, block, x1, h, on_pe, on_act, on_dve)


def fast_kinds(nc, ident, a8d, vw, unscale, x1, bias, spread_ok, bad, out):
    H = NB // 2
    HW = H * WB
    NBK = HW // 512
    with Phase(nc, "fk") as ph:
        a8 = ph.sb("a8", [P, 2, H, GW], F8)
        vs = ph.sb("vs", [P, 2, GT, 2, D], F16)
        junk_a = ph.sb("junk_a", [P, 2, GW], BF16)
        junk_d = ph.sb("junk_d", [P, 2, GW], BF16)
        sum_a, sum_d, all_a, all_d, ok_a, ok_d, ok, nok, worst = (
            ph.sb(n, [P, 1]) for n in ("sum_a", "sum_d", "all_a", "all_d", "ok_a", "ok_d", "ok", "nok", "worst"))
        oT = ph.sb("oT", [D, NBK, 512])
        rows = ph.sb("rows", [P, NBK, 4, D])
        bcol = ph.sb("bcol", [D, 1])
        half = ph.sb("half", [P, 1])
        acc = ph.ps("acc", [D, NBK, 512])

        def pair_of(name):
            return [ph.sem(f"{name}{b}") for b in range(2)]

        a8_in, staged, used, checked_a, checked_d = (
            pair_of(n) for n in ("a8_in", "staged", "used", "checked_a", "checked_d"))
        act_step, dve_step, pe_step, sp_step = (ph.sem(n) for n in ("act_step", "dve_step", "pe_step", "sp_step"))
        zeroed, added, x_in, b_in, moved, turned, summed, stored, judged, reduced = (
            ph.sem(n) for n in ("zeroed", "added", "x_in", "b_in", "moved", "turned", "summed", "stored", "judged",
                                "reduced"))
        src = a8d.rearrange("(s k g) p c -> s g p k c", s=2, k=H)
        x1t = x1.rearrange("(s c t p) d -> s p c t d", p=P, t=4, s=2)
        ot = out.rearrange("(s c t p) d -> s p c t d", p=P, t=4, s=2)
        PH = NG // 2
        with nc.Block() as block:
            @block.sync
            def _(sp):
                def load(s, q, b):
                    sp.dma_start(a8[:, b, :, :].bitcast(U8), src[s, bass.ds(q * 2 + b, 1), :, :, :].squeeze(0)
                                 ).then_inc(a8_in[b], 16)

                def refill(s, q, b):
                    m = s * PH + q + 1
                    sp.wait_ge(used[b], m)
                    sp.wait_ge(checked_a[b], m)
                    sp.wait_ge(checked_d[b], m)
                    sp.sem_inc(sp_step, 1)
                    load(s, q, b)

                for b in range(2):
                    sp.sem_inc(checked_a[b], 1)
                    sp.sem_inc(checked_d[b], 1)
                for s in range(2):
                    if s == 0:
                        for b in range(2):
                            load(0, 0, b)
                    else:
                        for b in range(2):
                            refill(1, 0, b)
                    with sp.Fori(1, PH) as q:
                        for b in range(2):
                            refill(s, q, b)

            @block.gpsimd
            def _(pool):
                pool.dma_start(bcol[:, :], bias.unsqueeze(1)).then_inc(b_in, 16)
                for s in range(2):
                    if s:
                        pool.wait_ge(stored, 16 * NBK)
                    pool.dma_start(rows[:, :, :, :], x1t[s]).then_inc(x_in, 16)
                pool.wait_ge(judged, 4)
                nc.gpsimd.partition_all_reduce(worst[:, :], nok[:, :], P, bass.bass_isa.ReduceOp.max
                                               ).then_inc(reduced, 1)

            @block.scalar
            def _(act):
                act.wait_ge(zeroed, 3)
                act.wait_ge(b_in, 16)
                for s in range(2):
                    with act.Fori(0, PH) as q:
                        for b in range(2):
                            m = q + s * PH
                            act.wait_ge(a8_in[b], (m + 1) * 16)
                            act.wait_ge(added, m * 2 + b + 1)
                            act.sem_inc(act_step, 1)
                            nc.scalar.activation(junk_a[:, :, :], a8[:, b, 0:2, :], ACT.Square, bias=half[:, 0:1],
                                                 accum_out=sum_a[:, 0:1]).then_inc(checked_a[b], 1)
                    act.wait_ge(used[1], (s + 1) * PH + 1)
                    for c in range(NBK):
                        nc.scalar.activation(oT[:, c, :], acc[:, c, :], ACT.Identity, bias=bcol[:, 0:1],
                                             scale=unscale[:, 0:1]).then_inc(moved, 1)
                    for c in range(NBK):
                        act.wait_ge(summed, s * NBK + c + 1)
                        act.dma_start(ot[s][:, c], rows[:, c, :, :]).then_inc(stored, 16)
                act.wait_ge(stored, 2 * NBK * 16)

            @block.vector
            def _(dve):
                nc.vector.memset(all_a[:, :], 0.0).then_inc(zeroed, 1)
                nc.vector.memset(all_d[:, :], 0.0).then_inc(zeroed, 1)
                nc.vector.memset(half[:, :], -0.5).then_inc(zeroed, 1)
                dve.wait_ge(zeroed, 3)
                dve.sem_inc(added, 1)
                for s in range(2):
                    with dve.Fori(0, PH) as q:
                        for b in range(2):
                            m = q + s * PH
                            dve.wait_ge(used[b], m + 1)
                            nc.vector.tensor_copy(vs[:, b, :, :, :].rearrange("p t k d -> p (t k d)"),
                                                  vw[:, bass.ds((q * 2 + b) * GT, GT), :, :]
                                                  .rearrange("p t k d -> p (t k d)")).then_inc(staged[b], 1)
                            dve.wait_ge(a8_in[b], (m + 1) * 16)
                            dve.wait_ge(zeroed, m * 2 + b + 3)
                            dve.sem_inc(dve_step, 1)
                            nc.vector.scalar_tensor_tensor(out=junk_d[:, :, :], in0=a8[:, b, 2:4, :], scalar=1.0,
                                                           in1=a8[:, b, 2:4, :], op0=ALU.subtract, op1=ALU.mult,
                                                           accum_out=sum_d[:, 0:1]).then_inc(checked_d[b], 1)
                            dve.wait_ge(checked_d[b], m + 2)
                            dve.wait_ge(checked_a[b], m + 2)
                            nc.vector.tensor_tensor(all_d[:, :], all_d[:, :], sum_d[:, :], ALU.add).then_inc(zeroed, 1)
                            nc.vector.tensor_tensor(all_a[:, :], all_a[:, :], sum_a[:, :], ALU.add).then_inc(added, 1)
                    dve.wait_ge(x_in, (s + 1) * 16)
                    for c in range(NBK):
                        dve.wait_ge(turned, s * NBK + c + 1)
                        nc.vector.tensor_tensor(rows[:, c, :, :], acc[:, c, :].rearrange("p (t d) -> p t d", d=D),
                                                rows[:, c, :, :], ALU.add).then_inc(summed, 1)
                dve.wait_ge(added, 2 * NG + 1)
                dve.wait_ge(zeroed, 3 + 2 * NG)
                nc.vector.tensor_scalar(ok_a[:, :], all_a[:, :], 0.25 * 2 * NG * 2 * GW, None,
                                        ALU.is_equal).then_inc(judged, 1)
                nc.vector.scalar_tensor_tensor(out=ok_d[:, :], in0=all_d[:, :], scalar=0.0, in1=spread_ok[:, :],
                                               op0=ALU.is_equal, op1=ALU.mult).then_inc(judged, 1)
                dve.wait_ge(judged, 2)
                nc.vector.tensor_tensor(ok[:, :], ok_a[:, :], ok_d[:, :], ALU.mult).then_inc(judged, 1)
                dve.wait_ge(judged, 3)
                nc.vector.tensor_scalar(nok[:, :], ok[:, :], -1.0, 1.0, ALU.mult, ALU.add).then_inc(judged, 1)
                dve.wait_ge(reduced, 1)
                nc.vector.tensor_copy(bad[:, :], worst[:, :]).then_inc(judged, 1)
                dve.wait_ge(judged, 5)

            @block.tensor
            def _(pe):
                for b in range(2):
                    pe.sem_inc(used[b], 1)

                def products(s, q, b, start):
                    m = q + s * PH
                    pe.wait_ge(staged[b], m + 1)
                    pe.wait_ge(a8_in[b], (m + 1) * 16)
                    pe.sem_inc(pe_step, 1)
                    for j in range(GT):
                        for part in range(2):
                            for c in range(NBK):
                                if start and s and j == 0 and part == 0:
                                    pe.wait_ge(summed, (s - 1) * NBK + c + 1)
                                last = nc.tensor.matmul(
                                    acc[:, c, :], vs[:, b, j, part, :],
                                    a8[:, b, c // 2, j * WB + (c % 2) * 512:j * WB + (c % 2 + 1) * 512],
                                    start=(start and j == 0 and part == 0), stop=False, skip_group_check=True)
                    last.then_inc(used[b], 1)

                for s in range(2):
                    products(s, 0, 0, True)
                    products(s, 0, 1, False)
                    with pe.Fori(1, PH) as q:
                        for b in range(2):
                            products(s, q, b, False)
                    for c in range(NBK):
                        pe.wait_ge(moved, s * NBK + c + 1)
                        for t in range(4):
                            last = nc.tensor.transpose(acc[:, c, t * P:(t + 1) * P], oT[:, c, t * P:(t + 1) * P],
                                                       ident[:, :])
                        last.then_inc(turned, 1)


def fast_layers(nc, ident, ones, x, adjG, a2, w1, bias, a8d, x1, out, bad):
    with Phase(nc, "fs") as ph:
        spread_ok = ph.sb("spread_ok", [P, 1])
        with Phase(nc, "f0") as p0:
            ef = p0.sb("ef", [P, NT, 2, 2, D1], F16)
            h1b = p0.sb("h1b", [P, N])
            mean_h = p0.sb("mean_h", [P, D])
            nh2, e1, f1 = (p0.sb(n, [P, NT]) for n in ("nh2", "e1", "f1"))
            with Phase(nc, "f1") as p1:
                h = p1.sb("h", [P, NT, D1])
                h1c, h2c = p1.sb("h1c", [P, NT]), p1.sb("h2c", [P, NT])
                scores_phase(nc, "fsc", ident, ones, x, a2, h, h1c, h2c, h1b, mean_h)
                factors_phase(nc, h, h1c, h2c, ef, nh2, e1, f1, spread_ok)
            fast_attention(nc, x, adjG, ef, nh2, e1, f1, h1b, mean_h, a8d, x1)
        with Phase(nc, "f2") as p2:
            vw = p2.sb("vw", [P, NT, 2, D], F16)
            unscale = p2.sb("unscale", [P, 1])
            fast_values(nc, ident, x1, w1, vw, unscale)
            fast_kinds(nc, ident, a8d, vw, unscale, x1, bias, spread_ok, bad, out)



def graph_layers(nc, x, adjG, a2, w1, w2, w3, bias, out):
    x1 = nc.dram_tensor("x1_scratch", (N, D), F32, kind="Internal").ap()
    a8d = nc.dram_tensor("a8_scratch", (NB * NG, P, GW), U8, kind="Internal").ap()
    with Phase(nc, "top") as ph:
        bad = ph.sb("bad", [P, 1], I32)
        ident, ones = constants(nc, ph)
        fast_layers(nc, ident, ones, x, adjG, a2, w1, bias, a8d, x1, out, bad)
        refused = nc.values_load(bad[0:1, 0:1], min_val=0, max_val=1)
        with nc.If(refused > 0):
            general_layers(nc, ident, ones, x, adjG, a2, [w1, w2, w3], bias, x1, out)


def kernel(x, adj, L0_gnn_a, L1_gnn_w1, L1_gnn_w2, L1_gnn_w3, L1_gnn_bias):
    import numpy as np
    import concourse.bacc as bacc
    from concourse.bass_utils import run_bass_kernel_spmd

    arrays = {
        "x": np.ascontiguousarray(x),
        "adjG": np.ascontiguousarray(np.asarray(adj).T.reshape(NG, GT, P, NB, WB).transpose(3, 0, 2, 1, 4)
                                     ).reshape(NB * NG, P, GT, WB),
        "a2": np.ascontiguousarray(np.asarray(L0_gnn_a).reshape(2, D).T),
        "w1": np.ascontiguousarray(L1_gnn_w1),
        "w2": np.ascontiguousarray(L1_gnn_w2),
        "w3": np.ascontiguousarray(L1_gnn_w3),
        "bias": np.ascontiguousarray(L1_gnn_bias),
    }
    nc = bacc.Bacc("TRN2", target_bir_lowering=False, num_devices=1)
    aps = {k: nc.dram_tensor(f"in_{k}", v.shape, mybir.dt.from_np(v.dtype), kind="ExternalInput").ap()
           for k, v in arrays.items()}
    out = nc.dram_tensor("out", (N, D), F32, kind="ExternalOutput").ap()
    graph_layers(nc, aps["x"], aps["adjG"], aps["a2"], aps["w1"], aps["w2"], aps["w3"], aps["bias"], out)
    r = run_bass_kernel_spmd(nc, [{f"in_{k}": v for k, v in arrays.items()}], core_ids=[0])
    return r.results[0]["out"]
```

```python
from contextlib import ExitStack

import concourse.bass as bass
from concourse import mybir

P = 128
N = 8192
D = 128
NT = N // P
WB = 1024
NB = N // WB
TB = WB // P
GT = 4
NG = NT // GT
GW = GT * WB
HG = GW // 2
NPAIR = NT // 2
MP = NB * NG // 2
D1 = D + 1
CH = 4
NCH = NT // CH
LC = 8
H = NB // 2
POOL_EVERY = 2
KC = LC // CH
NLC = NT // LC
EPS = 1e-5
SLOPE = 0.01
SPREAD = 8.0
SCALE = 4096.0
LOW = -3.0e38

F32 = mybir.dt.float32
F16 = mybir.dt.float16
BF16 = mybir.dt.bfloat16
F8 = mybir.dt.float8e4
U8 = mybir.dt.uint8
I32 = mybir.dt.int32
ALU = mybir.AluOpType
ACT = mybir.ActivationFunctionType
AX = mybir.AxisListType.X


class Adjacency:

    def __init__(self, ph, adjG):
        self.adjG = adjG
        self.raw = ph.sb("adj", [P, 2, GW], I32)
        self.a16 = ph.sb("a16", [P, 2, GW], F16)
        self.adj_in = [ph.sem(f"adj_in{b}") for b in range(2)]
        self.a16_ready = [ph.sem(f"a16_ready{b}") for b in range(2)]

    def load(self, sp, m, b, half):
        sp.dma_start(self.raw[:, b, half * HG:(half + 1) * HG],
                     self.adjG[bass.ds(m * 2 + b, 1), :, half * GT // 2:(half + 1) * GT // 2, :].squeeze(0)
                     .rearrange("p t w -> p (t w)")).then_inc(self.adj_in[b], 16)

    def convert_first(self, nc, act):
        for b in range(2):
            act.wait_ge(self.adj_in[b], 32)
            nc.scalar.activation(self.a16[:, b, :], self.raw[:, b, :], ACT.Sign).then_inc(self.a16_ready[b], 1)


class Copies:

    def __init__(self, ph, a8d):
        self.src = a8d.rearrange("(s k g) p c -> s g p k c", s=2, k=H)
        self.a8 = ph.sb("a8", [P, 2, H, GW], F8)
        self.a8_in = [ph.sem(f"a8_in{b}") for b in range(2)]

    def load(self, sp, s, q, b):
        sp.dma_start(self.a8[:, b, :, :].bitcast(U8), self.src[s, bass.ds(q * 2 + b, 1), :, :, :].squeeze(0)
                     ).then_inc(self.a8_in[b], 16)


class Rows:
    STEPS = 4
    WEIGH = 3

    def __init__(self, ph, x, x1):
        self.xt = x.rearrange("(i t p) d -> i p t d", p=P, t=TB)
        self.x1t = x1.rearrange("(i t p) d -> i p t d", p=P, t=TB)
        self.mean_h = ph.sb("mean_h", [P, D])
        self.num, self.tmp = ph.sb("num", [P, TB, D1]), ph.sb("tmp", [P, TB, D1])
        self.xin, self.fill = ph.sb("xin", [P, TB, D]), ph.sb("fill", [P, TB, D])
        self.alone, self.den, self.inv = (ph.sb(n, [P, TB]) for n in ("alone", "den", "inv"))
        self.x_in, self.x_out = ph.pool_dma_sem("x_in"), ph.pool_dma_sem("x_out")
        self.weighed, self.fin, self.x_go = (ph.sem(n) for n in ("weighed", "fin", "x_go"))

    def fetch(self, nc, pool, i):
        pool.wait_ge(self.fin, i * self.STEPS + 1)
        pool.sem_inc(self.x_go, 1)
        pool.dma_start(self.xin[:, :, :], self.xt[bass.ds(i, 1), :, :, :].squeeze(0)).then_inc(self.x_in, 16)

    def finish(self, nc, pool, i):
        tmp, xin, fill = self.tmp, self.xin, self.fill
        pool.wait_ge(self.weighed, (i + 1) * self.WEIGH)
        nc.gpsimd.tensor_tensor(tmp[:, :, 0:D], self.num[:, :, 0:D],
                                self.inv[:, :].unsqueeze(2).to_broadcast([P, TB, D]), ALU.mult).then_inc(self.fin, 1)
        nc.gpsimd.tensor_tensor(fill[:, :, :], self.mean_h[:, :].unsqueeze(1).to_broadcast([P, TB, D]),
                                self.alone[:, :].unsqueeze(2).to_broadcast([P, TB, D]),
                                ALU.mult).then_inc(self.fin, 1)
        pool.wait_ge(self.fin, i * self.STEPS + 3)
        pool.wait_ge(self.x_in, (i + 1) * 16)
        nc.gpsimd.tensor_tensor(tmp[:, :, 0:D], tmp[:, :, 0:D], fill[:, :, :], ALU.add).then_inc(self.fin, 1)
        pool.wait_ge(self.fin, i * self.STEPS + 4)
        nc.gpsimd.tensor_tensor(xin[:, :, :], tmp[:, :, 0:D], xin[:, :, :], ALU.add).then_inc(self.fin, 1)
        pool.wait_ge(self.fin, (i + 1) * self.STEPS + 1)
        pool.sem_inc(self.x_go, 1)
        pool.dma_start(self.x1t[bass.ds(i, 1), :, :, :].squeeze(0), xin[:, :, :]).then_inc(self.x_out, 16)


class Phase:

    def __init__(self, nc, name):
        self.nc, self.name, self.ctx = nc, name, ExitStack()

    def __enter__(self):
        self.ctx.__enter__()
        return self

    def __exit__(self, *a):
        return self.ctx.__exit__(*a)

    def sb(self, name, shape, dt=F32):
        return self.ctx.enter_context(self.nc.sbuf_tensor(f"{self.name}_{name}", shape, dt))

    def ps(self, name, shape, dt=F32):
        return self.ctx.enter_context(self.nc.psum_tensor(f"{self.name}_{name}", shape, dt))

    def sem(self, name):
        return self.ctx.enter_context(self.nc.semaphore(f"{self.name}_{name}"))

    def pool_dma_sem(self, name):
        return self.nc.alloc_semaphore(f"{self.name}_{name}")


def constants(nc, ph):
    ident = ph.sb("ident", [P, P])
    ones = ph.sb("ones", [P, P])
    cleared, made, filled = ph.sem("cleared"), ph.sem("made"), ph.sem("filled")
    with nc.Block() as block:
        @block.gpsimd
        def _(pool):
            nc.gpsimd.memset(ident[:, :], 0.0).then_inc(cleared, 1)
            pool.wait_ge(cleared, 1)
            nc.gpsimd.affine_select(out=ident[:, :], in_=ident[:, :], compare_op=ALU.not_equal, fill=1.0,
                                    base=0, pattern=[[-1, P]], channel_multiplier=1).then_inc(made, 1)
            pool.wait_ge(made, 1)

        @block.vector
        def _(dve):
            nc.vector.memset(ones[:, :], 1.0).then_inc(filled, 1)
            dve.wait_ge(filled, 1)
    return ident, ones



def normalise(nc, ph, block, src, h, on_pe, act_step, dve_step, dve_first=None, src_out=None, sp_last=None,
              LAG=3):
    stats = ph.sb("stats", [P, NT, nc.vector.BN_STATS_DIM])
    mv = ph.sb("mv", [P, NT, 2])
    var, std, rstd, shift = (ph.sb(n, [P, NT]) for n in ("var", "std", "rstd", "shift"))
    loaded = [ph.sem(f"loaded{c}") for c in range(NLC)]
    counted, averaged, biased, rooted, inverted, shifted, normed = (
        ph.sem(n) for n in ("counted", "averaged", "biased", "rooted", "inverted", "shifted", "normed"))
    tiles = src.rearrange("(t p) d -> p t d", p=P)

    def span(c):
        return slice(c * LC, (c + 1) * LC)

    @block.sync
    def _(sp):
        for c in range(NLC):
            if src_out is not None and c == NLC - 1:
                sp.wait_ge(src_out, NB * 16)
            sp.dma_start(h[:, span(c), 0:D], tiles[:, span(c), :]).then_inc(loaded[c], 16)
        if sp_last is not None:
            sp_last(sp)

    @block.scalar
    def _(act):
        for c in range(NLC + 2):
            if c < NLC:
                act.wait_ge(biased, c + 1)
                nc.scalar.activation(std[:, span(c)], var[:, span(c)], ACT.Sqrt).then_inc(rooted, 1)
            if 1 <= c <= NLC:
                act.wait_ge(shifted, c)
                for t in range((c - 1) * LC, c * LC):
                    nc.scalar.activation(h[:, t, 0:D], h[:, t, 0:D], ACT.Relu, bias=shift[:, t:t + 1],
                                         scale=rstd[:, t:t + 1]).then_inc(normed, 1)
            if c >= 2:
                for k in range((c - 2) * KC, (c - 1) * KC):
                    act_step(act, k)
        act_step(act, NCH)

    @block.vector
    def _(dve):
        for c in range(NLC + LAG):
            if c < NLC:
                dve.wait_ge(loaded[c], 16)
                for t in range(c * LC, (c + 1) * LC):
                    nc.vector.bn_stats(out=stats[:, t, :], in_=h[:, t, 0:D]).then_inc(counted, 1)
                for t in range(c * LC, (c + 1) * LC):
                    dve.wait_ge(counted, t + 1)
                    nc.vector.bn_aggr(out=mv[:, t, :], in_=stats[:, t, :]).then_inc(averaged, 1)
                dve.wait_ge(averaged, (c + 1) * LC)
                nc.vector.tensor_scalar(var[:, span(c)], mv[:, span(c), 1], EPS, None, ALU.add).then_inc(biased, 1)
            if c == 2 and dve_first:
                dve_first(dve)
            if 1 <= c <= NLC:
                dve.wait_ge(rooted, c)
                nc.vector.reciprocal(rstd[:, span(c - 1)], std[:, span(c - 1)]).then_inc(inverted, 1)
                dve.wait_ge(inverted, c)
                nc.vector.scalar_tensor_tensor(out=shift[:, span(c - 1)], in0=mv[:, span(c - 1), 0], scalar=-1.0,
                                               in1=rstd[:, span(c - 1)], op0=ALU.mult,
                                               op1=ALU.mult).then_inc(shifted, 1)
            if c >= LAG:
                for k in range((c - LAG) * KC, (c - LAG + 1) * KC):
                    dve_step(dve, k)
        dve_step(dve, NCH)

    @block.tensor
    def _(pe):
        on_pe(pe, normed)


def scores_phase(nc, name, ident, ones, x, a2, h, h1c, h2c, h1b, mean_h, edges=None):
    with Phase(nc, name) as ph:
        aw = ph.sb("aw", [D, 2])
        a1w = ph.sb("a1w", [D, P])
        nth = ph.sb("nth", [P, P])
        total = ph.sb("total", [P, LC, D])
        hT = ph.sb("hT", [D, 2, CH * P])
        pT = ph.ps("pT", [D, 2, CH * P])
        pH = ph.ps("pH", [P, 2, 512])
        pB = ph.ps("pB", [P, 2, CH * P])
        pM = ph.ps("pM", [P, 512])
        a_in = ph.pool_dma_sem("a_in")
        a_wide, turned, hT_ready, projected, spread, taken, copied, averaged_h, totalled = (
            ph.sem(n) for n in ("a_wide", "turned", "hT_ready", "projected", "spread", "taken",
                                "copied", "averaged_h", "totalled"))
        norm_seen, mean_out = ph.sem("norm_seen"), ph.sem("mean_out")
        with nc.Block() as block:
            def on_pe(pe, normed):
                pe.wait_ge(a_wide, 3)
                for k in range(NCH + 1):
                    if k < NCH:
                        pe.wait_ge(normed, (k + 1) * CH)
                        pe.sem_inc(norm_seen, 1)
                        if k >= 2:
                            pe.wait_ge(hT_ready, k - 1)
                        for t in range(CH):
                            last = nc.tensor.transpose(pT[:, k % 2, t * P:(t + 1) * P],
                                                       h[:, k * CH + t, 0:D], ident[:, :])
                        last.then_inc(turned, 1)
                    if k >= 1:
                        c = k - 1
                        pe.wait_ge(hT_ready, c + 1)
                        if c >= 2:
                            pe.wait_ge(taken, c - 1)
                            pe.wait_ge(copied, c - 1)
                        for t in range(CH):
                            last = nc.tensor.matmul(pH[:, c % 2, 2 * t:2 * t + 2],
                                                    hT[:, c % 2, t * P:(t + 1) * P], aw[:, :],
                                                    start=True, stop=True)
                        last.then_inc(projected, 1)
                        nc.tensor.matmul(pB[:, c % 2, :], a1w[:, :], hT[:, c % 2, :],
                                         start=True, stop=True).then_inc(spread, 1)
                pe.wait_ge(totalled, NLC)
                for t in range(LC):
                    last = nc.tensor.matmul(pM[:, 0:D], nth[:, :], total[:, t, :],
                                            start=(t == 0), stop=(t == LC - 1))
                last.then_inc(averaged_h, 1)

            def act_step(act, k):
                if k < NCH:
                    act.wait_ge(turned, k + 1)
                    if k >= 2:
                        act.wait_ge(spread, k - 1)
                    nc.scalar.activation(hT[:, k % 2, :], pT[:, k % 2, :], ACT.Copy).then_inc(hT_ready, 1)
                elif edges:
                    edges.convert_first(nc, act)

            def sp_last(sp):
                if edges:
                    for b in range(2):
                        for half in range(2):
                            edges.load(sp, 0, b, half)

            def dve_step(dve, k):
                if k == 0:
                    nc.vector.memset(h[:, :, D:D1], 1.0).then_inc(mean_out, 1)
                if k < NCH:
                    dve.wait_ge(projected, k + 1)
                    got = pH[:, k % 2, 0:2 * CH].rearrange("p (t k) -> p t k", k=2)
                    nc.vector.tensor_copy(h1c[:, k * CH:(k + 1) * CH], got[:, :, 0])
                    nc.vector.tensor_copy(h2c[:, k * CH:(k + 1) * CH], got[:, :, 1]).then_inc(taken, 1)
                    dve.wait_ge(spread, k + 1)
                    nc.vector.tensor_copy(h1b[:, k * CH * P:(k + 1) * CH * P], pB[:, k % 2, :]).then_inc(copied, 1)
                else:
                    dve.wait_ge(averaged_h, 1)
                    nc.vector.tensor_copy(mean_h[:, :], pM[:, 0:D]).then_inc(mean_out, 1)
                    dve.wait_ge(mean_out, 2)
                    dve.wait_ge(taken, NCH)
                    dve.wait_ge(copied, NCH)

            @block.gpsimd
            def _(pool):
                pool.dma_start(aw[:, :], a2).then_inc(a_in, 16)
                pool.wait_ge(a_in, 16)
                nc.gpsimd.tensor_scalar(a1w[:, :], ones[:, :], aw[:, 0:1], None, ALU.mult).then_inc(a_wide, 1)
                nc.gpsimd.memset(nth[:, :], 1.0 / N).then_inc(a_wide, 2)
                for c in range(NLC):
                    pool.wait_ge(norm_seen, (c + 1) * KC)
                    now = h[:, c * LC:(c + 1) * LC, 0:D]
                    if c == 0:
                        nc.gpsimd.tensor_copy(total[:, :, :], now).then_inc(totalled, 1)
                    else:
                        pool.wait_ge(totalled, c)
                        nc.gpsimd.tensor_tensor(total[:, :, :], total[:, :, :], now, ALU.add).then_inc(totalled, 1)

            normalise(nc, ph, block, x, h, on_pe, act_step, dve_step, sp_last=sp_last)


def general_maxima(nc, ident, ones, adjG, h1c, h2c, mb):
    with Phase(nc, "mx") as ph:
        adj = ph.sb("adj", [P, 2, WB], I32)
        off = ph.sb("off", [P, 2, WB])
        best = ph.sb("best", [P, WB])
        top = ph.sb("top", [P, NT])
        s = ph.sb("s", [P, NT])
        m = ph.sb("m", [P, NT])
        diag = ph.sb("diag", [P, 2, P])
        pR = ph.ps("pR", [P, TB, 128])
        pD = ph.ps("pD", [P, 2, 512])
        adj_in = [ph.sem(f"adj_in{b}") for b in range(2)]
        adj_used = [ph.sem(f"adj_used{b}") for b in range(2)]
        best_set, turned, topped, m_ready = (
            ph.sem(n) for n in ("best_set", "turned", "topped", "m_ready"))
        diag_ready = [ph.sem(f"diag_ready{b}") for b in range(2)]
        diag_used = [ph.sem(f"diag_used{b}") for b in range(2)]
        row_out = [ph.sem(f"row_out{b}") for b in range(2)]
        with nc.Block() as block:
            @block.sync
            def _(sp):
                for b in range(2):
                    sp.sem_inc(adj_used[b], 1)
                with sp.Fori(0, NB) as i:
                    with sp.Fori(0, NG) as g:
                        for j in range(GT):
                            q, b = g * 2 + j // 2, j % 2
                            sp.wait_ge(adj_used[b], i * NPAIR + q + 1)
                            sp.dma_start(adj[:, b, :], adjG[bass.ds(i * NG + g, 1), :, j, :].squeeze(0)
                                         ).then_inc(adj_in[b], 16)

            @block.vector
            def _(dve):
                dve.sem_inc(turned, 1)
                for b in range(2):
                    dve.sem_inc(diag_used[b], 1)
                with dve.Fori(0, NB) as i:
                    dve.wait_ge(turned, i + 1)
                    nc.vector.memset(best[:, :], LOW).then_inc(best_set, 1)
                    with dve.Fori(0, NPAIR) as q:
                        for b in range(2):
                            dve.wait_ge(adj_in[b], (i * NPAIR + q + 1) * 16)
                            nc.vector.tensor_scalar(off[:, b, :], adj[:, b, :], 0.0, LOW, ALU.is_le,
                                                    ALU.mult).then_inc(adj_used[b], 1)
                            dve.wait_ge(adj_used[b], i * NPAIR + q + 2)
                            dve.wait_ge(best_set, i * (2 * NPAIR + 1) + q * 2 + b + 1)
                            nc.vector.scalar_tensor_tensor(
                                out=best[:, :], in0=off[:, b, :], scalar=h2c[:, bass.ds(q * 2 + b, 1)],
                                in1=best[:, :], op0=ALU.add, op1=ALU.max).then_inc(best_set, 1)
                    dve.wait_ge(turned, i + 2)
                    nc.vector.reduce_max(top[:, bass.ds(i * TB, TB)], pR[:, :, :], AX).then_inc(topped, 1)
                dve.wait_ge(topped, NB + 1)
                nc.vector.tensor_tensor(s[:, :], h1c[:, :], top[:, :], ALU.add).then_inc(m_ready, 1)
                dve.wait_ge(m_ready, 1)
                nc.vector.scalar_tensor_tensor(out=m[:, :], in0=s[:, :], scalar=SLOPE, in1=s[:, :],
                                               op0=ALU.mult, op1=ALU.max).then_inc(m_ready, 1)
                dve.wait_ge(m_ready, 2)
                with dve.Fori(0, NPAIR) as q:
                    for b in range(2):
                        dve.wait_ge(diag_used[b], q + 1)
                        nc.vector.tensor_scalar(diag[:, b, :], ident[:, :], m[:, bass.ds(q * 2 + b, 1)], None,
                                                ALU.mult).then_inc(diag_ready[b], 1)

            @block.tensor
            def _(pe):
                pe.sem_inc(topped, 1)
                for b in range(2):
                    pe.sem_inc(row_out[b], 1)
                with pe.Fori(0, NB) as i:
                    pe.wait_ge(best_set, (i + 1) * (2 * NPAIR + 1))
                    pe.wait_ge(topped, i + 1)
                    for t in range(TB):
                        last = nc.tensor.transpose(pR[:, t, :], best[:, t * P:(t + 1) * P], ident[:, :])
                    last.then_inc(turned, 1)
                with pe.Fori(0, NPAIR) as q:
                    for b in range(2):
                        pe.wait_ge(diag_ready[b], q + 1)
                        pe.wait_ge(row_out[b], q + 1)
                        nc.tensor.matmul(pD[:, b, 0:P], ones[:, :], diag[:, b, :], start=True,
                                         stop=True).then_inc(diag_used[b], 1)

            @block.scalar
            def _(act):
                with act.Fori(0, NPAIR) as q:
                    for b in range(2):
                        act.wait_ge(diag_used[b], q + 2)
                        nc.scalar.activation(mb[:, bass.ds((q * 2 + b) * P, P)], pD[:, b, 0:P],
                                             ACT.Copy).then_inc(row_out[b], 1)


def general_attention(nc, x, adjG, h, h2c, h1b, mb, mean_h, x1):
    with Phase(nc, "at") as ph:
        adj = ph.sb("adj", [P, 2, WB], I32)
        z = ph.sb("z", [P, 2, WB])
        e = ph.sb("e", [P, 2, WB])
        dd = ph.sb("dd", [P, 2, WB])
        below = ph.sb("below", [P, 2, WB])
        w = ph.sb("w", [P, 2, WB])
        pw = ph.sb("pw", [P, 2, WB])
        acc = ph.ps("acc", [P, TB, 512])
        num = ph.sb("num", [P, TB, D1])
        alone, den, inv = (ph.sb(n, [P, TB]) for n in ("alone", "den", "inv"))
        part = ph.sb("part", [P, TB, D])
        mh = ph.sb("mh", [P, TB, D])
        xin = ph.sb("xin", [P, TB, D])
        adj_in = [ph.sem(f"adj_in{b}") for b in range(2)]
        w_ready = [ph.sem(f"w_ready{b}") for b in range(2)]
        d_ready = [ph.sem(f"d_ready{b}") for b in range(2)]
        b_ready = [ph.sem(f"b_ready{b}") for b in range(2)]
        p_ready = [ph.sem(f"p_ready{b}") for b in range(2)]
        p_used = [ph.sem(f"p_used{b}") for b in range(2)]
        z_ready, e_ready, drained, fin, x_in, x_out = (
            ph.sem(n) for n in ("z_ready", "e_ready", "drained", "fin", "x_in", "x_out"))
        FIN = 7
        xt = x.rearrange("(i t p) d -> i p t d", p=P, t=TB)
        x1t = x1.rearrange("(i t p) d -> i p t d", p=P, t=TB)
        with nc.Block() as block:
            @block.sync
            def _(sp):
                for b in range(2):
                    sp.sem_inc(p_ready[b], 1)
                with sp.Fori(0, NB) as i:
                    with sp.Fori(0, NG) as g:
                        for j in range(GT):
                            q, b = g * 2 + j // 2, j % 2
                            sp.wait_ge(p_ready[b], i * NPAIR + q + 1)
                            sp.dma_start(adj[:, b, :], adjG[bass.ds(i * NG + g, 1), :, j, :].squeeze(0)
                                         ).then_inc(adj_in[b], 16)

            @block.scalar
            def _(act):
                act.sem_inc(fin, 1)
                with act.Fori(0, NB) as i:
                    act.wait_ge(fin, i * FIN + 1)
                    act.dma_start(xin[:, :, :], xt[bass.ds(i, 1), :, :, :].squeeze(0)).then_inc(x_in, 16)
                    with act.Fori(0, NPAIR) as q:
                        for b in range(2):
                            n = i * NPAIR + q
                            act.wait_ge(d_ready[b], n + 1)
                            nc.scalar.activation(below[:, b, :], dd[:, b, :], ACT.Relu,
                                                 scale=-1.0).then_inc(b_ready[b], 1)
                            act.wait_ge(b_ready[b], n + 2)
                            act.wait_ge(p_ready[b], n + 1)
                            nc.scalar.activation(w[:, b, :], below[:, b, :], ACT.Exp,
                                                 scale=-1.0).then_inc(w_ready[b], 1)
                    act.wait_ge(fin, (i + 1) * FIN + 1)
                    act.dma_start(x1t[bass.ds(i, 1), :, :, :].squeeze(0), part[:, :, :]).then_inc(x_out, 16)
                    act.wait_ge(x_out, (i + 1) * 16)

            @block.vector
            def _(dve):
                for b in range(2):
                    dve.sem_inc(b_ready[b], 1)
                    dve.sem_inc(p_used[b], 1)
                with dve.Fori(0, NB) as i:
                    with dve.Fori(0, NPAIR) as q:
                        for b in range(2):
                            n = i * NPAIR + q
                            cols = bass.ds(i * WB, WB)
                            nc.vector.tensor_scalar(z[:, b, :], h1b[:, cols], h2c[:, bass.ds(q * 2 + b, 1)], None,
                                                    ALU.add).then_inc(z_ready, 1)
                            dve.wait_ge(z_ready, n * 2 + b + 1)
                            nc.vector.scalar_tensor_tensor(out=e[:, b, :], in0=z[:, b, :], scalar=SLOPE,
                                                           in1=z[:, b, :], op0=ALU.mult,
                                                           op1=ALU.max).then_inc(e_ready, 1)
                            dve.wait_ge(e_ready, n * 2 + b + 1)
                            dve.wait_ge(b_ready[b], n + 1)
                            nc.vector.tensor_tensor(dd[:, b, :], e[:, b, :], mb[:, cols],
                                                    ALU.subtract).then_inc(d_ready[b], 1)
                        for b in range(2):
                            n = i * NPAIR + q
                            dve.wait_ge(w_ready[b], n + 1)
                            dve.wait_ge(adj_in[b], (n + 1) * 16)
                            dve.wait_ge(p_used[b], n + 1)
                            nc.vector.scalar_tensor_tensor(out=pw[:, b, :], in0=adj[:, b, :], scalar=0.0,
                                                           in1=w[:, b, :], op0=ALU.is_gt,
                                                           op1=ALU.mult).then_inc(p_ready[b], 1)
                    dve.wait_ge(p_used[1], (i + 1) * NPAIR + 1)
                    nc.vector.tensor_copy(num[:, :, :], acc[:, :, 0:D1]).then_inc(drained, 1)
                    dve.wait_ge(drained, i + 2)
                    nc.vector.tensor_scalar(alone[:, :], num[:, :, D], 0.0, None, ALU.is_equal).then_inc(fin, 1)
                    dve.wait_ge(fin, i * FIN + 2)
                    nc.vector.tensor_tensor(den[:, :], num[:, :, D], alone[:, :], ALU.add).then_inc(fin, 1)
                    dve.wait_ge(fin, i * FIN + 3)
                    nc.vector.reciprocal(inv[:, :], den[:, :]).then_inc(fin, 1)
                    dve.wait_ge(fin, i * FIN + 4)
                    dve.wait_ge(x_in, (i + 1) * 16)
                    nc.vector.tensor_tensor(part[:, :, :], num[:, :, 0:D],
                                            inv[:, :].unsqueeze(2).to_broadcast([P, TB, D]), ALU.mult).then_inc(fin, 1)
                    nc.vector.tensor_tensor(mh[:, :, :], alone[:, :].unsqueeze(2).to_broadcast([P, TB, D]),
                                            mean_h[:, :].unsqueeze(1).to_broadcast([P, TB, D]),
                                            ALU.mult).then_inc(fin, 1)
                    dve.wait_ge(fin, i * FIN + 6)
                    nc.vector.tensor_tensor(part[:, :, :], part[:, :, :], mh[:, :, :], ALU.add).then_inc(fin, 1)
                    dve.wait_ge(fin, i * FIN + 7)
                    nc.vector.tensor_tensor(part[:, :, :], part[:, :, :], xin[:, :, :], ALU.add).then_inc(fin, 1)

            @block.tensor
            def _(pe):
                def step(i, q, b, first):
                    pe.wait_ge(p_ready[b], i * NPAIR + q + 2)
                    for t in range(TB):
                        last = nc.tensor.matmul(acc[:, t, 0:D1], pw[:, b, t * P:(t + 1) * P],
                                                h[:, bass.ds(q * 2 + b, 1), :].squeeze(1), start=first, stop=False,
                                                skip_group_check=True)
                    last.then_inc(p_used[b], 1)

                pe.sem_inc(drained, 1)
                with pe.Fori(0, NB) as i:
                    pe.wait_ge(drained, i + 1)
                    step(i, 0, 0, True)
                    step(i, 0, 1, False)
                    with pe.Fori(1, NPAIR) as q:
                        for b in range(2):
                            step(i, q, b, False)


def values_phase(nc, ident, x1, ws, h, vw):
    K = len(ws)
    with Phase(nc, "va") as ph:
        wt = ph.sb("wt", [D, K, D])
        hT = ph.sb("hT", [D, 2, CH * P])
        pT = ph.ps("pT", [D, 2, CH * P])
        pV = ph.ps("pV", [P, CH, 512])
        w_in = ph.pool_dma_sem("w_in")
        turned, hT_ready, projected, taken = (
            ph.sem(n) for n in ("turned", "hT_ready", "projected", "taken"))
        with nc.Block() as block:
            def on_pe(pe, normed):
                pe.wait_ge(w_in, 16 * K)
                for k in range(NCH + 1):
                    if k < NCH:
                        pe.wait_ge(normed, (k + 1) * CH)
                        if k >= 2:
                            pe.wait_ge(hT_ready, k - 1)
                        for t in range(CH):
                            last = nc.tensor.transpose(pT[:, k % 2, t * P:(t + 1) * P],
                                                       h[:, k * CH + t, 0:D], ident[:, :])
                        last.then_inc(turned, 1)
                    if k >= 1:
                        c = k - 1
                        pe.wait_ge(hT_ready, c + 1)
                        for t in range(CH):
                            if c >= 1:
                                pe.wait_ge(taken, (c - 1) * CH + t + 1)
                            nc.tensor.matmul(pV[:, t, 0:K * D], hT[:, c % 2, t * P:(t + 1) * P],
                                             wt[:, :, :].rearrange("p k d -> p (k d)"),
                                             start=True, stop=True).then_inc(projected, 1)

            def act_step(act, k):
                if k < NCH:
                    act.wait_ge(turned, k + 1)
                    if k >= 2:
                        act.wait_ge(projected, (k - 1) * CH)
                    nc.scalar.activation(hT[:, k % 2, :], pT[:, k % 2, :], ACT.Copy).then_inc(hT_ready, 1)

            def dve_step(dve, k):
                if k < NCH:
                    for n in range(k * CH, (k + 1) * CH):
                        dve.wait_ge(projected, n + 1)
                        nc.vector.tensor_copy(vw[:, n, :, :].rearrange("p k d -> p (k d)"),
                                              pV[:, n % CH, 0:K * D]).then_inc(taken, 1)
                else:
                    dve.wait_ge(taken, NT)

            @block.gpsimd
            def _(pool):
                for k in range(K):
                    pool.dma_start(wt[:, k, :], ws[k]).then_inc(w_in, 16)

            normalise(nc, ph, block, x1, h, on_pe, act_step, dve_step)


def general_kinds(nc, adjG, vw, x1, bias, out):
    K = 3
    with Phase(nc, "ki") as ph:
        adj = ph.sb("adj", [P, 2, WB], I32)
        mask = ph.sb("mask", [P, 2, K, WB])
        acc = ph.ps("acc", [P, TB, 512])
        res = ph.sb("res", [P, TB, D])
        xin = ph.sb("xin", [P, TB, D])
        brow = ph.sb("brow", [P, D])
        adj_in = [ph.sem(f"adj_in{b}") for b in range(2)]
        m_ready = [ph.sem(f"m_ready{b}") for b in range(2)]
        m_used = [ph.sem(f"m_used{b}") for b in range(2)]
        b_in, fin, x_in, x_out = (ph.sem(n) for n in ("b_in", "fin", "x_in", "x_out"))
        FIN = 2
        x1t = x1.rearrange("(i t p) d -> i p t d", p=P, t=TB)
        ot = out.rearrange("(i t p) d -> i p t d", p=P, t=TB)
        with nc.Block() as block:
            @block.sync
            def _(sp):
                for b in range(2):
                    sp.sem_inc(m_ready[b], 1)
                sp.dma_start(brow[:, :], bias.partition_broadcast(P)).then_inc(b_in, 16)
                with sp.Fori(0, NB) as i:
                    with sp.Fori(0, NG) as g:
                        for j in range(GT):
                            q, b = g * 2 + j // 2, j % 2
                            sp.wait_ge(m_ready[b], (i * NPAIR + q) * K + 1)
                            sp.dma_start(adj[:, b, :], adjG[bass.ds(i * NG + g, 1), :, j, :].squeeze(0)
                                         ).then_inc(adj_in[b], 16)

            @block.scalar
            def _(act):
                act.sem_inc(fin, 1)
                with act.Fori(0, NB) as i:
                    act.wait_ge(fin, i * FIN + 1)
                    act.dma_start(xin[:, :, :], x1t[bass.ds(i, 1), :, :, :].squeeze(0)).then_inc(x_in, 16)
                    act.wait_ge(fin, (i + 1) * FIN + 1)
                    act.dma_start(ot[bass.ds(i, 1), :, :, :].squeeze(0), res[:, :, :]).then_inc(x_out, 16)
                    act.wait_ge(x_out, (i + 1) * 16)

            @block.vector
            def _(dve):
                for b in range(2):
                    dve.sem_inc(m_used[b], 1)
                dve.wait_ge(b_in, 16)
                with dve.Fori(0, NB) as i:
                    with dve.Fori(0, NPAIR) as q:
                        for b in range(2):
                            n = i * NPAIR + q
                            dve.wait_ge(adj_in[b], (n + 1) * 16)
                            dve.wait_ge(m_used[b], n + 1)
                            for k in range(K):
                                nc.vector.tensor_scalar(mask[:, b, k, :], adj[:, b, :], float(k + 1), None,
                                                        ALU.is_equal).then_inc(m_ready[b], 1)
                    dve.wait_ge(m_used[1], (i + 1) * NPAIR + 1)
                    dve.wait_ge(x_in, (i + 1) * 16)
                    nc.vector.tensor_tensor(res[:, :, :], acc[:, :, 0:D], xin[:, :, :], ALU.add).then_inc(fin, 1)
                    dve.wait_ge(fin, i * FIN + 2)
                    nc.vector.tensor_tensor(res[:, :, :], res[:, :, :],
                                            brow[:, :].unsqueeze(1).to_broadcast([P, TB, D]),
                                            ALU.add).then_inc(fin, 1)

            @block.tensor
            def _(pe):
                def step(i, q, b, first):
                    pe.wait_ge(m_ready[b], (i * NPAIR + q + 1) * K + 1)
                    for t in range(TB):
                        for k in range(K):
                            last = nc.tensor.matmul(acc[:, t, 0:D], mask[:, b, k, t * P:(t + 1) * P],
                                                    vw[:, bass.ds(q * 2 + b, 1), k, :].squeeze(1),
                                                    start=(first and k == 0), stop=False, skip_group_check=True)
                    last.then_inc(m_used[b], 1)

                with pe.Fori(0, NB) as i:
                    pe.wait_ge(fin, i * FIN + 1)
                    step(i, 0, 0, True)
                    step(i, 0, 1, False)
                    with pe.Fori(1, NPAIR) as q:
                        for b in range(2):
                            step(i, q, b, False)


def general_layers(nc, ident, ones, x, adjG, a2, ws, bias, x1, out):
    with Phase(nc, "ge") as ph:
        with Phase(nc, "g0") as p0:
            h = p0.sb("h", [P, NT, D1])
            h1c, h2c = p0.sb("h1c", [P, NT]), p0.sb("h2c", [P, NT])
            mean_h = p0.sb("mean_h", [P, D])
            h1b = p0.sb("h1b", [P, N])
            scores_phase(nc, "gs", ident, ones, x, a2, h, h1c, h2c, h1b, mean_h)
            mb = p0.sb("mb", [P, N])
            general_maxima(nc, ident, ones, adjG, h1c, h2c, mb)
            general_attention(nc, x, adjG, h, h2c, h1b, mb, mean_h, x1)
        with Phase(nc, "g1") as p1:
            vw = p1.sb("vw", [P, NT, 3, D])
            with Phase(nc, "g2") as p2:
                h = p2.sb("h", [P, NT, D])
                values_phase(nc, ident, x1, ws, h, vw)
            general_kinds(nc, adjG, vw, x1, bias, out)


def factors_phase(nc, h, h1c, h2c, ef, nh2, e1, f1, spread_ok, edges):
    with Phase(nc, "fa") as ph:
        ends = ph.sb("ends", [P, 2])
        top = ph.sb("top", [P, 2])
        width, off = ph.sb("width", [P, 1]), ph.sb("off", [P, NT])
        z, zs, lo, hi = (ph.sb(n, [P, NT]) for n in ("z", "zs", "lo", "hi"))
        src = ph.sb("src", [P, 2, NT])
        srcs = ph.sb("srcs", [P, 2, NT])
        ended, topped, bound, made, exped, scaled, upper, upper_pool, lower = (
            ph.sem(n) for n in ("ended", "topped", "bound", "made", "exped", "scaled", "upper", "upper_pool",
                                "lower"))
        with nc.Block() as block:
            @block.gpsimd
            def _(pool):
                pool.wait_ge(ended, 3)
                nc.gpsimd.partition_all_reduce(top[:, :], ends[:, :], P, bass.bass_isa.ReduceOp.max
                                               ).then_inc(topped, 1)
                pool.wait_ge(scaled, 1)
                for t in range(0, NT, POOL_EVERY):
                    nc.gpsimd.tensor_scalar(ef[:, t, 0, 0, :], h[:, t, :], srcs[:, 0, t:t + 1], None,
                                            ALU.mult).then_inc(upper_pool, 1)

            @block.vector
            def _(dve):
                nc.vector.tensor_scalar(nh2[:, :], h2c[:, :], -1.0, None, ALU.mult).then_inc(ended, 1)
                nc.vector.reduce_max(ends[:, 0:1], h2c[:, :], AX).then_inc(ended, 1)
                dve.wait_ge(ended, 2)
                nc.vector.reduce_max(ends[:, 1:2], nh2[:, :], AX).then_inc(ended, 1)
                dve.wait_ge(topped, 1)
                nc.vector.tensor_tensor(width[:, :], top[:, 0:1], top[:, 1:2], ALU.add).then_inc(made, 1)
                nc.vector.tensor_scalar(z[:, :], h1c[:, :], top[:, 0:1], 1.0 - SLOPE, ALU.add,
                                        ALU.mult).then_inc(made, 1)
                dve.wait_ge(made, 2)
                nc.vector.tensor_scalar(spread_ok[:, :], width[:, :], SPREAD, None, ALU.is_le).then_inc(made, 1)
                nc.vector.tensor_scalar(lo[:, :], z[:, :], 0.0, None, ALU.min).then_inc(made, 1)
                nc.vector.tensor_scalar(hi[:, :], z[:, :], 0.0, 2 * SPREAD, ALU.max, ALU.min).then_inc(made, 1)
                nc.vector.tensor_scalar(off[:, :], h2c[:, :], top[:, 0:1], -2 * SPREAD, ALU.subtract,
                                        ALU.max).then_inc(bound, 1)
                dve.wait_ge(made, 5)
                dve.wait_ge(exped, 2)
                nc.vector.tensor_scalar(srcs[:, :, :], src[:, :, :], SCALE, None, ALU.mult).then_inc(scaled, 1)
                dve.wait_ge(scaled, 1)
                for t in range(NT):
                    for k in range(2):
                        by_pool = t // POOL_EVERY + 1
                        if k == 0 and t % POOL_EVERY == 0:
                            dve.wait_ge(upper_pool, by_pool)
                        else:
                            dve.wait_ge(upper, t * 2 + k + 1 - by_pool)
                        nc.vector.scalar_tensor_tensor(
                            out=ef[:, t, k, 1, :], in0=h[:, t, :], scalar=srcs[:, k, t:t + 1],
                            in1=ef[:, t, k, 0, :], op0=ALU.mult, op1=ALU.subtract).then_inc(lower, 1)
                dve.wait_ge(lower, 2 * NT)

            @block.scalar
            def _(act):
                act.wait_ge(bound, 1)
                nc.scalar.activation(src[:, 0, :], off[:, :], ACT.Exp).then_inc(exped, 1)
                nc.scalar.activation(src[:, 1, :], off[:, :], ACT.Exp, scale=SLOPE).then_inc(exped, 1)
                act.wait_ge(made, 5)
                nc.scalar.activation(e1[:, :], lo[:, :], ACT.Exp).then_inc(exped, 1)
                nc.scalar.activation(f1[:, :], hi[:, :], ACT.Exp, scale=-1.0).then_inc(exped, 1)
                act.wait_ge(exped, 4)
                act.wait_ge(scaled, 1)
                for t in range(NT):
                    for k in range(2):
                        if k or t % POOL_EVERY:
                            nc.scalar.activation(ef[:, t, k, 0, :], h[:, t, :], ACT.Copy,
                                                 scale=srcs[:, k, t:t + 1]).then_inc(upper, 1)


def fast_attention(nc, edges, ef, nh2, e1, f1, h1b, a8d, rows):
    with Phase(nc, "fl") as ph:
        adj, a16, adj_in, a16_ready = edges.raw, edges.a16, edges.adj_in, edges.a16_ready
        a8 = ph.sb("a8", [P, 2, GW], F8)
        above = ph.sb("above", [P, 2, GW], F16)
        under = ph.sb("under", [P, 2, GW], F16)
        num, tmp, alone, den, inv = rows.num, rows.tmp, rows.alone, rows.den, rows.inv
        fin, weighed, FIN, WEIGH = rows.fin, rows.weighed, rows.STEPS, rows.WEIGH
        acc = ph.ps("acc", [P, TB, 512])

        def pair_of(name):
            return [ph.sem(f"{name}{b}") for b in range(2)]

        a8_half, a8_ready, a8_out, above_ready, under_ready, used = (
            pair_of(n) for n in ("a8_half", "a8_ready", "a8_out", "above_ready", "under_ready", "used"))
        below_out, drained, act_step = (ph.sem(n) for n in ("below_out", "drained", "act_step"))
        PB = NG // 2
        with nc.Block() as block:
            @block.sync
            def _(sp):
                def store(m, b):
                    sp.dma_start(a8d[bass.ds(m * 2 + b, 1), :, :].squeeze(0), a8[:, b, :].bitcast(U8)
                                 ).then_inc(a8_out[b], 16)

                with sp.Fori(1, MP) as m:
                    for b in range(2):
                        sp.wait_ge(a16_ready[b], m)
                        sp.wait_ge(a8_half[b], m)
                        edges.load(sp, m, b, 0)
                        sp.wait_ge(a8_ready[b], m)
                        edges.load(sp, m, b, 1)
                        store(m - 1, b)
                for b in range(2):
                    sp.wait_ge(a8_ready[b], MP)
                    store(MP - 1, b)
                for b in range(2):
                    sp.wait_ge(a8_out[b], MP * 16)

            @block.scalar
            def _(act):
                def convert(m, b, first):
                    act.wait_ge(adj_in[b], (m + 1) * 32)
                    if not first:
                        act.wait_ge(under_ready[b], m * 2)
                        nc.scalar.activation(a16[:, b, :], adj[:, b, :], ACT.Sign).then_inc(a16_ready[b], 1)
                        act.wait_ge(a8_out[b], m * 16)
                    act.sem_inc(act_step, 1)
                    nc.scalar.activation(a8[:, b, 0:HG], adj[:, b, 0:HG], ACT.Copy, saturate=True
                                         ).then_inc(a8_half[b], 1)
                    nc.scalar.activation(a8[:, b, HG:GW], adj[:, b, HG:GW], ACT.Copy, saturate=True
                                         ).then_inc(a8_ready[b], 1)

                def drain_under(i):
                    act.wait_ge(used[1], (i + 1) * PB * 2)
                    act.wait_ge(fin, i * FIN + 1)
                    act.sem_inc(act_step, 1)
                    for t in range(TB):
                        nc.scalar.activation(tmp[:, t, :], acc[:, t, D1:2 * D1], ACT.Copy,
                                             scale=f1[:, bass.ds(i * TB + t, 1)]).then_inc(below_out, 1)

                for b in range(2):
                    convert(0, b, True)
                def rest(i):
                    for b in range(2):
                        convert(i * PB + 1, b, False)
                    with act.Fori(1, PB // 2) as u:
                        for q in range(2):
                            for b in range(2):
                                convert(i * PB + u * 2 + q, b, False)

                with act.Fori(0, NB - 1) as i:
                    rest(i)
                    convert((i + 1) * PB, 0, False)
                    drain_under(i)
                    convert((i + 1) * PB, 1, False)
                rest(NB - 1)
                drain_under(NB - 1)

            @block.gpsimd
            def _(pool):
                pool.sem_inc(fin, 1)
                with pool.Fori(0, NB - 1) as i:
                    rows.fetch(nc, pool, i)
                    rows.finish(nc, pool, i)
                    pool.wait_ge(rows.x_out, (i + 1) * 16)
                    pool.sem_inc(rows.x_go, 1)
                rows.fetch(nc, pool, NB - 1)

            @block.vector
            def _(dve):
                def split(i, q, b, first, between=None):
                    m = i * PB + q
                    dve.wait_ge(a16_ready[b], m + 1)
                    for half in range(2):
                        if not first:
                            dve.wait_ge(used[b], m * 2 + half - 1)
                        for j in range(half * GT // 2, (half + 1) * GT // 2):
                            cols = slice(j * WB, (j + 1) * WB)
                            nc.vector.scalar_tensor_tensor(
                                out=above[:, b, cols], in0=h1b[:, bass.ds(i * WB, WB)],
                                scalar=nh2[:, bass.ds((q * 2 + b) * GT + j, 1)], in1=a16[:, b, cols],
                                op0=ALU.is_gt, op1=ALU.mult).then_inc(above_ready[b], 1)
                        dve.wait_ge(above_ready[b], (m * 2 + half + 1) * (GT // 2))
                        cols = slice(half * HG, (half + 1) * HG)
                        nc.vector.tensor_tensor(under[:, b, cols], a16[:, b, cols], above[:, b, cols],
                                                ALU.subtract).then_inc(under_ready[b], 1)
                        if between and half == 0:
                            between()

                def drain(i):
                    dve.wait_ge(used[1], (i + 1) * PB * 2)
                    dve.wait_ge(fin, i * FIN + 1)
                    for t in range(TB):
                        dve.wait_ge(below_out, i * TB + t + 1)
                        nc.vector.scalar_tensor_tensor(
                            out=num[:, t, :], in0=acc[:, t, 0:D1], scalar=e1[:, bass.ds(i * TB + t, 1)],
                            in1=tmp[:, t, :], op0=ALU.mult, op1=ALU.add).then_inc(drained, 1)

                def weigh(i):
                    dve.wait_ge(drained, (i + 2) * TB)
                    nc.vector.tensor_scalar(alone[:, :], num[:, :, D], 0.0, None, ALU.is_equal).then_inc(weighed, 1)
                    dve.wait_ge(weighed, i * WEIGH + 1)
                    nc.vector.tensor_tensor(den[:, :], num[:, :, D], alone[:, :], ALU.add).then_inc(weighed, 1)
                    dve.wait_ge(weighed, i * WEIGH + 2)
                    nc.vector.reciprocal(inv[:, :], den[:, :]).then_inc(weighed, 1)

                def rest(i):
                    for b in range(2):
                        split(i, 1, b, False)
                    with dve.Fori(1, PB // 2) as u:
                        for q in range(2):
                            for b in range(2):
                                split(i, u * 2 + q, b, False)

                for b in range(2):
                    split(0, 0, b, True)
                with dve.Fori(0, NB - 1) as i:
                    rest(i)
                    split(i + 1, 0, 0, False, lambda: drain(i))
                    split(i + 1, 0, 1, False)
                    weigh(i)
                rest(NB - 1)
                drain(NB - 1)
                weigh(NB - 1)

            @block.tensor
            def _(pe):
                def products(i, q, b, start):
                    for j in range(GT):
                        if j % (GT // 2) == 0:
                            pe.wait_ge(under_ready[b], (i * PB + q) * 2 + j // (GT // 2) + 1)
                        for t in range(TB):
                            if start and j == 0:
                                pe.wait_ge(drained, i * TB + t + 1)
                            cols = slice(j * WB + t * P, j * WB + (t + 1) * P)
                            for k, mask in enumerate((above, under)):
                                for part in range(2):
                                    last = nc.tensor.matmul(
                                        acc[:, t, k * D1:(k + 1) * D1], mask[:, b, cols],
                                        ef[:, bass.ds((q * 2 + b) * GT + j, 1), k, part, :].squeeze(1),
                                        start=(start and j == 0 and k == 0 and part == 0), stop=False,
                                        skip_group_check=True)
                        if j % (GT // 2) == GT // 2 - 1:
                            last.then_inc(used[b], 1)

                pe.sem_inc(drained, TB)
                with pe.Fori(0, NB) as i:
                    for q in range(2):
                        for b in range(2):
                            products(i, q, b, q + b == 0)
                    with pe.Fori(1, PB // 2) as u:
                        for q in range(2):
                            for b in range(2):
                                products(i, u * 2 + q, b, False)


def fast_values(nc, ident, x1, rows, w1, vw, unscale, copies):
    VB = 4
    with Phase(nc, "fv") as ph:
        h = ph.sb("h", [P, NT, D])
        wt = ph.sb("wt", [D, D])
        wneg = ph.sb("wneg", [D, D])
        ends, top = ph.sb("ends", [P, 2]), ph.sb("top", [P, 2])
        big, power, inverse, scale = (ph.sb(n, [P, 1]) for n in ("big", "power", "inverse", "scale"))
        hT = ph.sb("hT", [D, 2, CH * P])
        pT = ph.ps("pT", [D, 2, CH * P])
        pV = ph.ps("pV", [P, VB, CH * P])
        w_in = ph.pool_dma_sem("w_in")
        ended, topped, scaled, turned, hT_ready, projected, upper, lower = (
            ph.sem(n) for n in ("ended", "topped", "scaled", "turned", "hT_ready", "projected", "upper",
                                "lower"))
        with nc.Block() as block:
            @block.gpsimd
            def _(pool):
                pool.dma_start(wt[:, :], w1).then_inc(w_in, 16)
                rows.finish(nc, pool, NB - 1)
                pool.wait_ge(ended, 3)
                nc.gpsimd.partition_all_reduce(top[:, :], ends[:, :], P, bass.bass_isa.ReduceOp.max
                                               ).then_inc(topped, 1)

            def on_pe(pe, normed):
                pe.wait_ge(w_in, 16)
                for k in range(NCH + 1):
                    if k < NCH:
                        pe.wait_ge(normed, (k + 1) * CH)
                        if k >= 2:
                            pe.wait_ge(hT_ready, k - 1)
                        for t in range(CH):
                            last = nc.tensor.transpose(pT[:, k % 2, t * P:(t + 1) * P],
                                                       h[:, k * CH + t, 0:D], ident[:, :])
                        last.then_inc(turned, 1)
                    if k >= 1:
                        c = k - 1
                        pe.wait_ge(hT_ready, c + 1)
                        if c >= VB:
                            pe.wait_ge(lower, c - VB + 1)
                        for t in range(CH):
                            last = nc.tensor.matmul(pV[:, c % VB, t * P:(t + 1) * P],
                                                    hT[:, c % 2, t * P:(t + 1) * P], wt[:, :],
                                                    start=True, stop=True)
                        last.then_inc(projected, 1)

            def act_step(act, k):
                if k < NCH:
                    act.wait_ge(turned, k + 1)
                    if k >= 2:
                        act.wait_ge(projected, k - 1)
                    nc.scalar.activation(hT[:, k % 2, :], pT[:, k % 2, :], ACT.Copy).then_inc(hT_ready, 1)
                if k >= 1:
                    c = k - 1
                    if c == 0:
                        act.wait_ge(scaled, 5)
                    act.wait_ge(projected, c + 1)
                    nc.scalar.activation(vw[:, c * CH:(c + 1) * CH, 0, :],
                                         pV[:, c % VB, :].rearrange("p (t d) -> p t d", d=D), ACT.Copy,
                                         scale=scale[:, 0:1]).then_inc(upper, 1)

            def dve_first(dve):
                dve.wait_ge(w_in, 16)
                nc.vector.reduce_max(ends[:, 0:1], wt[:, :], AX).then_inc(ended, 1)
                nc.vector.tensor_scalar(wneg[:, :], wt[:, :], -1.0, None, ALU.mult).then_inc(ended, 1)
                dve.wait_ge(ended, 2)
                nc.vector.reduce_max(ends[:, 1:2], wneg[:, :], AX).then_inc(ended, 1)
                dve.wait_ge(topped, 1)
                nc.vector.tensor_scalar(big[:, :], top[:, 0:1], top[:, 1:2], 1e-30, ALU.max,
                                        ALU.max).then_inc(scaled, 1)
                dve.wait_ge(scaled, 1)
                nc.vector.tensor_scalar(power[:, :].bitcast(I32), big[:, :].bitcast(I32), 0x7F800000, None,
                                        ALU.bitwise_and).then_inc(scaled, 1)
                dve.wait_ge(scaled, 2)
                nc.vector.reciprocal(inverse[:, :], power[:, :]).then_inc(scaled, 1)
                nc.vector.tensor_scalar(unscale[:, :], power[:, :], 1.0 / D, None, ALU.mult).then_inc(scaled, 1)
                dve.wait_ge(scaled, 4)
                nc.vector.tensor_scalar(scale[:, :], inverse[:, :], float(D), None, ALU.mult).then_inc(scaled, 1)
                dve.wait_ge(scaled, 5)

            def dve_step(dve, k):
                if k < NCH:
                    dve.wait_ge(upper, k + 1)
                    nc.vector.scalar_tensor_tensor(
                        out=vw[:, k * CH:(k + 1) * CH, 1, :], in0=pV[:, k % VB, :].rearrange("p (t d) -> p t d", d=D),
                        scalar=scale[:, 0:1], in1=vw[:, k * CH:(k + 1) * CH, 0, :], op0=ALU.mult,
                        op1=ALU.subtract).then_inc(lower, 1)
                else:
                    dve.wait_ge(lower, NCH)

            def sp_last(sp):
                for b in range(2):
                    copies.load(sp, 0, 0, b)

            normalise(nc, ph, block, x1, h, on_pe, act_step, dve_step, dve_first, rows.x_out, sp_last,
                      LAG=4)


def fast_kinds(nc, ident, copies, vw, unscale, x1, bias, spread_ok, bad, out):
    NBK = H * WB // 512
    with Phase(nc, "fk") as ph:
        a8, a8_in = copies.a8, copies.a8_in
        vs = ph.sb("vs", [P, 2, GT, 2, D], F16)
        junk_a = ph.sb("junk_a", [P, 2, GW], BF16)
        junk_d = ph.sb("junk_d", [P, 2, GW], BF16)
        sum_a, sum_d, all_a, all_d, ok_a, ok_d, ok, nok, worst = (
            ph.sb(n, [P, 1]) for n in ("sum_a", "sum_d", "all_a", "all_d", "ok_a", "ok_d", "ok", "nok", "worst"))
        oT = ph.sb("oT", [D, NBK, 512])
        rows = ph.sb("rows", [P, NBK, 4, D])
        bcol = ph.sb("bcol", [D, 1])
        half = ph.sb("half", [P, 1])
        acc = ph.ps("acc", [D, NBK, 512])

        def pair_of(name):
            return [ph.sem(f"{name}{b}") for b in range(2)]

        staged, used, checked_a, checked_d = (
            pair_of(n) for n in ("staged", "used", "checked_a", "checked_d"))
        act_step, dve_step, pe_step, sp_step = (ph.sem(n) for n in ("act_step", "dve_step", "pe_step", "sp_step"))
        x_in, b_in = ph.pool_dma_sem("x_in"), ph.pool_dma_sem("b_in")
        zeroed, added, moved, turned, summed, stored, judged, reduced = (
            ph.sem(n) for n in ("zeroed", "added", "moved", "turned", "summed", "stored", "judged",
                                "reduced"))
        x1t = x1.rearrange("(s c t p) d -> s p c t d", p=P, t=4, s=2)
        ot = out.rearrange("(s c t p) d -> s p c t d", p=P, t=4, s=2)
        PH = NG // 2
        with nc.Block() as block:
            @block.sync
            def _(sp):
                def refill(s, q, b):
                    m = s * PH + q + 1
                    sp.wait_ge(used[b], m)
                    sp.wait_ge(checked_a[b], m)
                    sp.wait_ge(checked_d[b], m)
                    sp.sem_inc(sp_step, 1)
                    copies.load(sp, s, q, b)

                for b in range(2):
                    sp.sem_inc(checked_a[b], 1)
                    sp.sem_inc(checked_d[b], 1)
                for s in range(2):
                    if s:
                        for b in range(2):
                            refill(1, 0, b)
                    with sp.Fori(1, PH) as q:
                        for b in range(2):
                            refill(s, q, b)

            @block.gpsimd
            def _(pool):
                pool.dma_start(bcol[:, :], bias.unsqueeze(1)).then_inc(b_in, 16)
                for s in range(2):
                    if s:
                        pool.wait_ge(stored, 16 * NBK)
                    pool.dma_start(rows[:, :, :, :], x1t[s]).then_inc(x_in, 16)
                pool.wait_ge(judged, 4)
                nc.gpsimd.partition_all_reduce(worst[:, :], nok[:, :], P, bass.bass_isa.ReduceOp.max
                                               ).then_inc(reduced, 1)

            @block.scalar
            def _(act):
                act.wait_ge(zeroed, 3)
                act.wait_ge(b_in, 16)
                for s in range(2):
                    with act.Fori(0, PH) as q:
                        for b in range(2):
                            m = q + s * PH
                            act.wait_ge(a8_in[b], (m + 1) * 16)
                            act.wait_ge(added, m * 2 + b + 1)
                            act.sem_inc(act_step, 1)
                            nc.scalar.activation(junk_a[:, :, :], a8[:, b, 0:2, :], ACT.Square, bias=half[:, 0:1],
                                                 accum_out=sum_a[:, 0:1]).then_inc(checked_a[b], 1)
                    act.wait_ge(used[1], (s + 1) * PH + 1)
                    for c in range(NBK):
                        nc.scalar.activation(oT[:, c, :], acc[:, c, :], ACT.Identity, bias=bcol[:, 0:1],
                                             scale=unscale[:, 0:1]).then_inc(moved, 1)
                    for c in range(NBK):
                        act.wait_ge(summed, s * NBK + c + 1)
                        act.dma_start(ot[s][:, c], rows[:, c, :, :]).then_inc(stored, 16)
                act.wait_ge(stored, 2 * NBK * 16)

            @block.vector
            def _(dve):
                def judge():
                    dve.wait_ge(added, 2 * NG + 1)
                    dve.wait_ge(zeroed, 3 + 2 * NG)
                    nc.vector.tensor_scalar(ok_a[:, :], all_a[:, :], 0.25 * 2 * NG * 2 * GW, None,
                                            ALU.is_equal).then_inc(judged, 1)
                    nc.vector.scalar_tensor_tensor(out=ok_d[:, :], in0=all_d[:, :], scalar=0.0, in1=spread_ok[:, :],
                                                   op0=ALU.is_equal, op1=ALU.mult).then_inc(judged, 1)
                    dve.wait_ge(judged, 2)
                    nc.vector.tensor_tensor(ok[:, :], ok_a[:, :], ok_d[:, :], ALU.mult).then_inc(judged, 1)
                    dve.wait_ge(judged, 3)
                    nc.vector.tensor_scalar(nok[:, :], ok[:, :], -1.0, 1.0, ALU.mult, ALU.add).then_inc(judged, 1)

                nc.vector.memset(all_a[:, :], 0.0).then_inc(zeroed, 1)
                nc.vector.memset(all_d[:, :], 0.0).then_inc(zeroed, 1)
                nc.vector.memset(half[:, :], -0.5).then_inc(zeroed, 1)
                dve.wait_ge(zeroed, 3)
                dve.sem_inc(added, 1)
                for s in range(2):
                    with dve.Fori(0, PH) as q:
                        for b in range(2):
                            m = q + s * PH
                            dve.wait_ge(used[b], m + 1)
                            nc.vector.tensor_copy(vs[:, b, :, :, :].rearrange("p t k d -> p (t k d)"),
                                                  vw[:, bass.ds((q * 2 + b) * GT, GT), :, :]
                                                  .rearrange("p t k d -> p (t k d)")).then_inc(staged[b], 1)
                            dve.wait_ge(a8_in[b], (m + 1) * 16)
                            dve.wait_ge(zeroed, m * 2 + b + 3)
                            dve.sem_inc(dve_step, 1)
                            nc.vector.scalar_tensor_tensor(out=junk_d[:, :, :], in0=a8[:, b, 2:4, :], scalar=1.0,
                                                           in1=a8[:, b, 2:4, :], op0=ALU.subtract, op1=ALU.mult,
                                                           accum_out=sum_d[:, 0:1]).then_inc(checked_d[b], 1)
                            dve.wait_ge(checked_d[b], m + 2)
                            dve.wait_ge(checked_a[b], m + 2)
                            nc.vector.tensor_tensor(all_d[:, :], all_d[:, :], sum_d[:, :], ALU.add).then_inc(zeroed, 1)
                            nc.vector.tensor_tensor(all_a[:, :], all_a[:, :], sum_a[:, :], ALU.add).then_inc(added, 1)
                    if s == 1:
                        judge()
                    dve.wait_ge(x_in, (s + 1) * 16)
                    for c in range(NBK):
                        dve.wait_ge(turned, s * NBK + c + 1)
                        nc.vector.tensor_tensor(rows[:, c, :, :], acc[:, c, :].rearrange("p (t d) -> p t d", d=D),
                                                rows[:, c, :, :], ALU.add).then_inc(summed, 1)
                dve.wait_ge(reduced, 1)
                nc.vector.tensor_copy(bad[:, :], worst[:, :]).then_inc(judged, 1)
                dve.wait_ge(judged, 5)

            @block.tensor
            def _(pe):
                for b in range(2):
                    pe.sem_inc(used[b], 1)

                def products(s, q, b, start):
                    m = q + s * PH
                    pe.wait_ge(staged[b], m + 1)
                    pe.wait_ge(a8_in[b], (m + 1) * 16)
                    pe.sem_inc(pe_step, 1)
                    for j in range(GT):
                        for part in range(2):
                            for c in range(NBK):
                                if start and s and j == 0 and part == 0:
                                    pe.wait_ge(summed, (s - 1) * NBK + c + 1)
                                last = nc.tensor.matmul(
                                    acc[:, c, :], vs[:, b, j, part, :],
                                    a8[:, b, c // 2, j * WB + (c % 2) * 512:j * WB + (c % 2 + 1) * 512],
                                    start=(start and j == 0 and part == 0), stop=False, skip_group_check=True)
                    last.then_inc(used[b], 1)

                for s in range(2):
                    products(s, 0, 0, True)
                    products(s, 0, 1, False)
                    with pe.Fori(1, PH) as q:
                        for b in range(2):
                            products(s, q, b, False)
                    for c in range(NBK):
                        pe.wait_ge(moved, s * NBK + c + 1)
                        for t in range(4):
                            last = nc.tensor.transpose(acc[:, c, t * P:(t + 1) * P], oT[:, c, t * P:(t + 1) * P],
                                                       ident[:, :])
                        last.then_inc(turned, 1)


def fast_layers(nc, ident, ones, x, adjG, a2, w1, bias, a8d, x1, out, bad):
    with Phase(nc, "fs") as ph:
        spread_ok = ph.sb("spread_ok", [P, 1])
        rows = Rows(ph, x, x1)
        with Phase(nc, "f0") as p0:
            ef = p0.sb("ef", [P, NT, 2, 2, D1], F16)
            h1b = p0.sb("h1b", [P, N])
            nh2, e1, f1 = (p0.sb(n, [P, NT]) for n in ("nh2", "e1", "f1"))
            edges = Adjacency(p0, adjG)
            with Phase(nc, "f1") as p1:
                h = p1.sb("h", [P, NT, D1])
                h1c, h2c = p1.sb("h1c", [P, NT]), p1.sb("h2c", [P, NT])
                scores_phase(nc, "fsc", ident, ones, x, a2, h, h1c, h2c, h1b, rows.mean_h, edges)
                factors_phase(nc, h, h1c, h2c, ef, nh2, e1, f1, spread_ok, edges)
            fast_attention(nc, edges, ef, nh2, e1, f1, h1b, a8d, rows)
        with Phase(nc, "f2") as p2:
            vw = p2.sb("vw", [P, NT, 2, D], F16)
            unscale = p2.sb("unscale", [P, 1])
            copies = Copies(p2, a8d)
            fast_values(nc, ident, x1, rows, w1, vw, unscale, copies)
            fast_kinds(nc, ident, copies, vw, unscale, x1, bias, spread_ok, bad, out)



def clear_semaphores(nc):
    free = nc.free_semaphores
    with nc.Block() as block:
        @block.gpsimd
        def _(pool):
            pool.sem_clear(range(min(free), max(free) + 1))

        @block.vector
        def _(dve):
            dve.nop()

        @block.scalar
        def _(act):
            act.nop()

        @block.tensor
        def _(pe):
            pe.nop()

        @block.sync
        def _(sp):
            sp.nop()


def graph_layers(nc, x, adjG, a2, w1, w2, w3, bias, out):
    x1 = nc.dram_tensor("x1_scratch", (N, D), F32, kind="Internal").ap()
    a8d = nc.dram_tensor("a8_scratch", (NB * NG, P, GW), U8, kind="Internal").ap()
    with Phase(nc, "top") as ph:
        bad = ph.sb("bad", [P, 1], I32)
        ident, ones = constants(nc, ph)
        fast_layers(nc, ident, ones, x, adjG, a2, w1, bias, a8d, x1, out, bad)
        refused = nc.values_load(bad[0:1, 0:1], min_val=0, max_val=1)
        with nc.If(refused > 0):
            clear_semaphores(nc)
            general_layers(nc, ident, ones, x, adjG, a2, [w1, w2, w3], bias, x1, out)


def kernel(x, adj, L0_gnn_a, L1_gnn_w1, L1_gnn_w2, L1_gnn_w3, L1_gnn_bias):
    import numpy as np
    import concourse.bacc as bacc
    from concourse.bass_utils import run_bass_kernel_spmd

    arrays = {
        "x": np.ascontiguousarray(x),
        "adjG": np.ascontiguousarray(np.asarray(adj).T.reshape(NG, GT, P, NB, WB).transpose(3, 0, 2, 1, 4)
                                     ).reshape(NB * NG, P, GT, WB),
        "a2": np.ascontiguousarray(np.asarray(L0_gnn_a).reshape(2, D).T),
        "w1": np.ascontiguousarray(L1_gnn_w1),
        "w2": np.ascontiguousarray(L1_gnn_w2),
        "w3": np.ascontiguousarray(L1_gnn_w3),
        "bias": np.ascontiguousarray(L1_gnn_bias),
    }
    nc = bacc.Bacc("TRN2", target_bir_lowering=False, num_devices=1)
    aps = {k: nc.dram_tensor(f"in_{k}", v.shape, mybir.dt.from_np(v.dtype), kind="ExternalInput").ap()
           for k, v in arrays.items()}
    out = nc.dram_tensor("out", (N, D), F32, kind="ExternalOutput").ap()
    graph_layers(nc, aps["x"], aps["adjG"], aps["a2"], aps["w1"], aps["w2"], aps["w3"], aps["bias"], out)
    r = run_bass_kernel_spmd(nc, [{f"in_{k}": v for k, v in arrays.items()}], core_ids=[0])
    return r.results[0]["out"]
```
